# Optimizing a Trainium2 kernel written in Bass

```python
import numpy as np
import jax
import jax.numpy as jnp

def _softmax(x, axis=-1):
    return jax.nn.softmax(x, axis=axis)

def _gelu(x):
    return jax.nn.gelu(x, approximate=True)

def _silu(x):
    return jax.nn.silu(x)

def _sigmoid(x):
    return jax.nn.sigmoid(x)

def _layernorm(x, axis=-1, eps=1e-05):
    m = jnp.mean(x, axis=axis, keepdims=True)
    v = jnp.var(x, axis=axis, keepdims=True)
    return (x - m) / jnp.sqrt(v + eps)

def _scatter_add(tgt, idx, src, axis=0):
    return tgt.at[idx].add(src)

def _segment_sum(src, seg, n):
    return jax.ops.segment_sum(src, seg, n)
kernel_name = 'mk_macaron_d1_jaxref_r8_69a994'

def setup_inputs(seed: int=0):
    np.random.seed(seed)
    _w = jnp.asarray

    def _L0_attn_setup():
        import jax, jax.numpy as jnp
        import numpy as np
        EMBED_DIM = 128
        LAMBDA_INIT = 0.8
        EPS = 1e-05
        key = jax.random.key(seed)
        ks = jax.random.split(key, 8)
        D = EMBED_DIM
        x = jax.random.normal(ks[0], (4, 256, D), dtype=jnp.float32)
        s = 1.0 / np.sqrt(D)
        w_q12 = jax.random.uniform(ks[1], (D, 2 * D), jnp.float32, -s, s)
        w_k12 = jax.random.uniform(ks[2], (D, 2 * D), jnp.float32, -s, s)
        w_v = jax.random.uniform(ks[3], (D, D), jnp.float32, -s, s)
        lambda_q1 = 0.1 * jax.random.normal(ks[4], (D,), jnp.float32)
        lambda_k1 = 0.1 * jax.random.normal(ks[5], (D,), jnp.float32)
        lambda_q2 = 0.1 * jax.random.normal(ks[6], (D,), jnp.float32)
        lambda_k2 = 0.1 * jax.random.normal(ks[7], (D,), jnp.float32)
        return {'x': x, 'w_q12': w_q12, 'w_k12': w_k12, 'w_v': w_v, 'lambda_q1': lambda_q1, 'lambda_k1': lambda_k1, 'lambda_q2': lambda_q2, 'lambda_k2': lambda_k2}
    _L0_attn_in = _L0_attn_setup()

    def _L0_ffn_setup():
        import jax, jax.numpy as jnp
        import numpy as np
        DIM = 128
        INTER = 128
        E = 8
        TOPK = 2
        ROUTE_SCALE = 1.0
        SHARED_INTER = 256
        B, S = (4, 256)

        def _moe_forward(x, gate_w, gate_b, w1, b1, w3, b3, w2, b2, ws1, bs1, ws3, bs3, ws2, bs2):
            Bq, Sq, D = x.shape
            xt = x.reshape(-1, D)
            logits = (xt @ gate_w.T + gate_b).astype(jnp.float32)
            scores = jax.nn.softmax(logits, axis=-1)
            top_w, top_i = jax.lax.top_k(scores, TOPK)
            weights = (top_w * ROUTE_SCALE).astype(x.dtype)
            gate_dense = jnp.sum(jax.nn.one_hot(top_i, E, dtype=x.dtype) * weights[..., None], axis=1)

            def expert(w1e, b1e, w3e, b3e, w2e, b2e):
                h = jax.nn.silu(xt @ w1e.T + b1e) * (xt @ w3e.T + b3e)
                return h @ w2e.T + b2e
            outs = jax.vmap(expert)(w1, b1, w3, b3, w2, b2)
            y = jnp.einsum('etd,te->td', outs, gate_dense)
            z = jax.nn.silu(xt @ ws1.T + bs1) * (xt @ ws3.T + bs3) @ ws2.T + bs2
            return (y + z).reshape(Bq, Sq, D)
        key = jax.random.key(seed)
        ks = jax.random.split(key, 10)

        def w(k, shape, scale=0.02):
            return jax.random.normal(k, shape, jnp.float32) * scale
        return {'x': jax.random.normal(ks[0], (B, S, DIM), jnp.float32), 'gate_w': w(ks[1], (E, DIM)), 'gate_b': jnp.zeros((E,), jnp.float32), 'w1': w(ks[2], (E, INTER, DIM)), 'b1': jnp.zeros((E, INTER), jnp.float32), 'w3': w(ks[3], (E, INTER, DIM)), 'b3': jnp.zeros((E, INTER), jnp.float32), 'w2': w(ks[4], (E, DIM, INTER)), 'b2': jnp.zeros((E, DIM), jnp.float32), 'ws1': w(ks[5], (SHARED_INTER, DIM)), 'bs1': jnp.zeros((SHARED_INTER,), jnp.float32), 'ws3': w(ks[6], (SHARED_INTER, DIM)), 'bs3': jnp.zeros((SHARED_INTER,), jnp.float32), 'ws2': w(ks[7], (DIM, SHARED_INTER)), 'bs2': jnp.zeros((DIM,), jnp.float32)}
    _L0_ffn_in = _L0_ffn_setup()
    _d = {'L0_attn_x': _L0_attn_in['x'], 'L0_attn_w_q12': _L0_attn_in['w_q12'], 'L0_attn_w_k12': _L0_attn_in['w_k12'], 'L0_attn_w_v': _L0_attn_in['w_v'], 'L0_attn_lambda_q1': _L0_attn_in['lambda_q1'], 'L0_attn_lambda_k1': _L0_attn_in['lambda_k1'], 'L0_attn_lambda_q2': _L0_attn_in['lambda_q2'], 'L0_attn_lambda_k2': _L0_attn_in['lambda_k2'], 'L0_ffn_gate_w': _L0_ffn_in['gate_w'], 'L0_ffn_gate_b': _L0_ffn_in['gate_b'], 'L0_ffn_w1': _L0_ffn_in['w1'], 'L0_ffn_b1': _L0_ffn_in['b1'], 'L0_ffn_w3': _L0_ffn_in['w3'], 'L0_ffn_b3': _L0_ffn_in['b3'], 'L0_ffn_w2': _L0_ffn_in['w2'], 'L0_ffn_b2': _L0_ffn_in['b2'], 'L0_ffn_ws1': _L0_ffn_in['ws1'], 'L0_ffn_bs1': _L0_ffn_in['bs1'], 'L0_ffn_ws3': _L0_ffn_in['ws3'], 'L0_ffn_bs3': _L0_ffn_in['bs3'], 'L0_ffn_ws2': _L0_ffn_in['ws2'], 'L0_ffn_bs2': _L0_ffn_in['bs2']}
    _x0 = _d['L0_attn_x']
    _d['L0_attn_x'] = jax.random.normal(jax.random.fold_in(jax.random.key(seed), 1), (1, 2048, 128), dtype=_x0.dtype)
    del _x0
    return _d

def reference(L0_attn_x, L0_attn_w_q12, L0_attn_w_k12, L0_attn_w_v, L0_attn_lambda_q1, L0_attn_lambda_k1, L0_attn_lambda_q2, L0_attn_lambda_k2, L0_ffn_gate_w, L0_ffn_gate_b, L0_ffn_w1, L0_ffn_b1, L0_ffn_w3, L0_ffn_b3, L0_ffn_w2, L0_ffn_b2, L0_ffn_ws1, L0_ffn_bs1, L0_ffn_ws3, L0_ffn_bs3, L0_ffn_ws2, L0_ffn_bs2):

    def _L0_attn_ref(x, w_q12, w_k12, w_v, lambda_q1, lambda_k1, lambda_q2, lambda_k2):
        import jax, jax.numpy as jnp
        import numpy as np
        EMBED_DIM = 128
        LAMBDA_INIT = 0.8
        EPS = 1e-05
        D = x.shape[-1]
        scale = D ** (-0.25)
        q12 = jnp.einsum('bsd,de->bse', x, w_q12)
        k12 = jnp.einsum('bsd,de->bse', x, w_k12)
        q1, q2 = jnp.split(q12, 2, axis=-1)
        k1, k2 = jnp.split(k12, 2, axis=-1)
        v = jnp.einsum('bsd,de->bse', x, w_v)
        attn1 = jnp.einsum('bqd,bkd->bqk', q1, k1) * scale
        attn2 = jnp.einsum('bqd,bkd->bqk', q2, k2) * scale
        lam1 = jnp.exp(jnp.sum(lambda_q1 * lambda_k1))
        lam2 = jnp.exp(jnp.sum(lambda_q2 * lambda_k2))
        lam_full = lam1 - lam2 + LAMBDA_INIT
        diff = jax.nn.softmax(attn1, axis=-1) - lam_full * jax.nn.softmax(attn2, axis=-1)
        out = jnp.einsum('bqk,bkd->bqd', diff, v)
        rms = jnp.sqrt(jnp.mean(out * out, axis=-1, keepdims=True) + EPS)
        return out / rms * (1.0 - LAMBDA_INIT)

    def _L0_ffn_ref(x, gate_w, gate_b, w1, b1, w3, b3, w2, b2, ws1, bs1, ws3, bs3, ws2, bs2):
        import jax, jax.numpy as jnp
        import numpy as np
        DIM = 128
        INTER = 128
        E = 8
        TOPK = 2
        ROUTE_SCALE = 1.0
        SHARED_INTER = 256
        B, S = (4, 256)

        def _moe_forward(x, gate_w, gate_b, w1, b1, w3, b3, w2, b2, ws1, bs1, ws3, bs3, ws2, bs2):
            Bq, Sq, D = x.shape
            xt = x.reshape(-1, D)
            logits = (xt @ gate_w.T + gate_b).astype(jnp.float32)
            scores = jax.nn.softmax(logits, axis=-1)
            top_w, top_i = jax.lax.top_k(scores, TOPK)
            weights = (top_w * ROUTE_SCALE).astype(x.dtype)
            gate_dense = jnp.sum(jax.nn.one_hot(top_i, E, dtype=x.dtype) * weights[..., None], axis=1)

            def expert(w1e, b1e, w3e, b3e, w2e, b2e):
                h = jax.nn.silu(xt @ w1e.T + b1e) * (xt @ w3e.T + b3e)
                return h @ w2e.T + b2e
            outs = jax.vmap(expert)(w1, b1, w3, b3, w2, b2)
            y = jnp.einsum('etd,te->td', outs, gate_dense)
            z = jax.nn.silu(xt @ ws1.T + bs1) * (xt @ ws3.T + bs3) @ ws2.T + bs2
            return (y + z).reshape(Bq, Sq, D)
        return _moe_forward(x, gate_w, gate_b, w1, b1, w3, b3, w2, b2, ws1, bs1, ws3, bs3, ws2, bs2)
    x = L0_attn_x
    x = x + 0.5 * _L0_ffn_ref(_layernorm(x, axis=-1), L0_ffn_gate_w, L0_ffn_gate_b, L0_ffn_w1, L0_ffn_b1, L0_ffn_w3, L0_ffn_b3, L0_ffn_w2, L0_ffn_b2, L0_ffn_ws1, L0_ffn_bs1, L0_ffn_ws3, L0_ffn_bs3, L0_ffn_ws2, L0_ffn_bs2)
    x = x + _L0_attn_ref(_layernorm(x, axis=-1), L0_attn_w_q12, L0_attn_w_k12, L0_attn_w_v, L0_attn_lambda_q1, L0_attn_lambda_k1, L0_attn_lambda_q2, L0_attn_lambda_k2)
    x = x + 0.5 * _L0_ffn_ref(_layernorm(x, axis=-1), L0_ffn_gate_w, L0_ffn_gate_b, L0_ffn_w1, L0_ffn_b1, L0_ffn_w3, L0_ffn_b3, L0_ffn_w2, L0_ffn_b2, L0_ffn_ws1, L0_ffn_bs1, L0_ffn_ws3, L0_ffn_bs3, L0_ffn_ws2, L0_ffn_bs2)
    return x

_drawn_inputs = setup_inputs


def setup_inputs(seed=0):
    import zlib

    import numpy as np

    out = dict(_drawn_inputs(seed))
    spreads = {'L0_ffn_gate_b': (0.0, 0.577),
     'L0_ffn_b1': (0.0, 0.8),
     'L0_ffn_b3': (0.0, 0.8),
     'L0_ffn_b2': (0.0, 0.363),
     'L0_ffn_bs1': (0.0, 0.8),
     'L0_ffn_bs3': (0.0, 0.8),
     'L0_ffn_bs2': (0.0, 0.1)}
    factors = {'L0_attn_lambda_q1': 8.0,
     'L0_attn_lambda_q2': 6.757,
     'L0_attn_lambda_k2': 3.026,
     'L0_ffn_gate_w': 3.004,
     'L0_ffn_w1': 8.0,
     'L0_ffn_w3': 8.0,
     'L0_ffn_w2': 8.0,
     'L0_ffn_ws1': 6.398,
     'L0_ffn_ws3': 6.324,
     'L0_ffn_ws2': 5.778}
    for name, (base, spread) in spreads.items():
        noise = np.random.default_rng([zlib.crc32(name.encode()), seed]).standard_normal(out[name].shape)
        drawn = base * np.exp(spread * noise) if base else spread * noise
        out[name] = jnp.asarray(drawn.astype(out[name].dtype))
    for name, factor in factors.items():
        out[name] = (out[name] * factor).astype(out[name].dtype)
    return out
```

```python
from contextlib import ExitStack

import concourse.bass as bass
from concourse import mybir
from concourse.alu_op_type import AluOpType as ALU

F32 = mybir.dt.float32
F32R = mybir.dt.float32r
ACT = mybir.ActivationFunctionType
AX_X = mybir.AxisListType.X

P = 128
TOP = 2


def macaron(nc, x_in, w_units, cols_in, gate_b, b2_rows, attn_w, lambdas, out):
    T, D = x_in.shape
    E = gate_b.shape[1]
    NT = T // P
    BT = 4
    BLK = BT * P
    NB = NT // BT
    NU = w_units.shape[1] // (3 * P)
    NSH = NU - E
    GT_ = 2
    GRP = GT_ * P
    NG = NT // GT_
    CH = BLK
    NCH = T // CH
    HALF = T // 2
    assert D == P and T == NB * BLK and NCH == 4 and NB * 2 == NG
    SCALE = float(D) ** -0.25
    EPS = 1e-5
    LAMBDA_INIT = 0.8
    LAG = 3
    HR = 4
    WR = 3
    WCH = 2
    NWC = NU // WCH
    ONE, LOW = 2 * E, 32
    GR = LOW + E + 1
    BHI, BLO = 2 * E + 1, E + 1

    with ExitStack() as ctx:
        def sb(name, shape, dt=F32):
            return ctx.enter_context(nc.sbuf_tensor(name, shape, dt))

        def sem(name):
            return ctx.enter_context(nc.semaphore(name))

        WORD = 4
        ARENA = (4 * NT * GRP + 3 * T) * WORD
        ARENA0 = (nc.sbuf_base + 31) // 32 * 32
        sb("arena", [P, ARENA // WORD + 8])

        x = sb("x", [P, NT, D])
        xt_high = [sb(f"xt_high{i}", [P, T], F32R) for i in range(2)]
        xt_low = [sb(f"xt_low{i}", [P, T], F32R) for i in range(2)]
        w_high = sb("w_high", [P, NU, 3, P], F32R)
        w_low = sb("w_low", [P, NU, 3, P], F32R)
        v_high = sb("v_high", [P, NT, D], F32R)
        v_low = sb("v_low", [P, NT, D], F32R)
        gates_t = sb("gates_t", [P, T], F32R)
        gate_rows = sb("gate_rows", [P, (NT - 1) * GR + P])
        pick = sb("pick", [P, E, P], F32R)
        q_high = sb("q_high", [P, 2, 2 * GRP], F32R)
        q_low = sb("q_low", [P, 2, 2 * GRP], F32R)
        a_high = sb("a_high", [P, 2, P], F32R)
        a_low = sb("a_low", [P, 2, P], F32R)
        b2_st = sb("b2_st", [P, P], F32R)
        gw_high = sb("gw_high", [P, E], F32R)
        gw_low = sb("gw_low", [P, E], F32R)
        ident = sb("ident", [P, P])
        cols = sb("cols", [P, 2 * NU + E])
        b1 = lambda u: cols[:, u:u + 1]
        b3 = lambda u: cols[:, NU + u:NU + u + 1]
        gb = sb("gb", [P, E])
        rank = sb("rank", [P, E])
        mhalf = sb("mhalf", [P, BT])
        stats = sb("stats", [P, BT, 6])
        mv = sb("mv", [P, BT, 2])
        ve, y0, ya, rstd = (sb(n, [P, BT]) for n in ("ve", "y0", "ya", "rstd"))
        xn = sb("xn", [P, BT, D])
        z, ez, g1, g2 = (sb(n, [P, NT, E]) for n in ("z", "ez", "g1", "g2"))
        g_high = sb("g_high", [P, NT, E], F32R)
        gs = sb("gs", [P, NT])
        lam_s, lam_e = sb("lam_s", [P, 2]), sb("lam_e", [P, 2])
        neg_lam = sb("neg_lam", [P, 1])
        o_s = sb("o_s", [P, GRP])
        o_tok = sb("o_tok", [P, GT_, D])
        ssq, f1, f2, f3 = (sb(n, [P, GT_]) for n in ("ssq", "f1", "f2", "f3"))
        maxes = sb("maxes", [P, 2, 2])
        neg_m = sb("neg_m", [P, 2, 2])
        sums = sb("sums", [P, 2, 2, 2])
        total = sb("total", [P, 2])
        r2 = sb("r2", [P, 1])
        r1 = sb("r1", [P, NT])
        neg_c = sb("neg_c", [P, 1])


        def at(name, shape, word, dt=F32):
            size = 1
            for k in shape[1:]:
                size *= k
            assert (word + size) * WORD <= ARENA
            return nc.alloc_sbuf_tensor_at(name, shape, dt, offset=ARENA0 + word * WORD), word + size

        dt_parts, w = at("dt_parts", [P, 2, 2, NT, GRP], 0, F32R)
        p_rows, w = at("p_rows", [P, 3, T], w)
        w_raw, w = at("w_raw", [P, NU, 3, P], 0)
        aw_raw, w = at("aw_raw", [P, 5, P], w)
        aw_high, w = at("aw_high", [P, 5, P], w, F32R)
        aw_low, w = at("aw_low", [P, 5, P], w, F32R)
        b2_raw, w = at("b2_raw", [P, P], w)
        b2_high, w = at("b2_high", [P, P], w, F32R)
        lam_in, w = at("lam_in", [P, 4, D], w)
        lam_prod, w = at("lam_prod", [P, 2, D], w)
        out_s, w = at("out_s", [P, BLK], w)
        h_ring, w = at("h_ring", [P, HR, 2, BLK], w, F32R)
        silu_ring, w = at("silu_ring", [P, 2, BLK], w)
        prod_ring, w = at("prod_ring", [P, 2, BLK], w)
        gated_ring, w = at("gated_ring", [P, WR, BLK], w)
        h_high = lambda u: h_ring[:, u % HR, 0, :]
        h_low = lambda u: h_ring[:, u % HR, 1, :]
        silu_s = lambda u: silu_ring[:, u % 2, :]
        prod_s = lambda u: prod_ring[:, u % 2, :]
        gated = lambda u: gated_ring[:, u % WR, :]

        slots = [ctx.enter_context(nc.psum_tensor(f"slot{i}", [P, 2 * BLK], F32)) for i in range(3)]
        turn = ctx.enter_context(nc.psum_tensor("turn", [P, BLK], F32))
        single = ctx.enter_context(nc.psum_tensor("single", [P, BLK], F32))
        ps_h1 = lambda u: slots[0][:, (u % 2) * BLK:(u % 2 + 1) * BLK]
        ps_h3 = lambda u: slots[1][:, (u % 2) * BLK:(u % 2 + 1) * BLK]
        ps_out = lambda b: slots[2][:, (b % 2) * BLK:(b % 2 + 1) * BLK]

        x_in_s = [sem(f"x_in{b}") for b in range(NB)]
        w_in_s = [sem(f"w_in{c}") for c in range(NWC)]
        aw_in_s, cols_in_s, gb_in_s, b2_in_s, lam_in_s = (sem(n) for n in ("aw_in", "cols_in", "gb_in", "b2_in", "lam_in_s"))
        out_stored = sem("out_stored")
        pool_const = sem("pool_const")
        w_high_done, w_low_done = sem("w_high_done"), sem("w_low_done")
        gw_high_done, gw_low_done = sem("gw_high_done"), sem("gw_low_done")
        aw_high_done, aw_low_done = sem("aw_high_done"), sem("aw_low_done")
        b2_high_done, b2_low_done = sem("b2_high_done"), sem("b2_low_done")
        turn_full, logits_read = sem("turn_full"), sem("logits_read")
        ve_ready, pow_done, xn_ready = sem("ve_ready"), sem("pow_done"), sem("xn_ready")
        xt_high_done, xt_low_done = sem("xt_high_done"), sem("xt_low_done")
        z_ready, ez_done, gate_rows_ready, gates_t_done = (sem(n) for n in ("z_ready", "ez_done", "gate_rows_ready", "gates_t_done"))
        h1_full, h3_full, gb_full = sem("h1_full"), sem("h3_full"), sem("gb_full")
        silu_done, prod_done, gated_done = sem("silu_done"), sem("prod_done"), sem("gated_done")
        h_high_done, h_low_done, second_done = sem("h_high_done"), sem("h_low_done"), sem("second_done")
        out_full, out_s_done = sem("out_full"), sem("out_s_done")
        ffn_added, attn_added = sem("ffn_added"), sem("attn_added")
        a_high_done, a_low_done = sem("a_high_done"), sem("a_low_done")
        v_high_done, v_low_done = sem("v_high_done"), sem("v_low_done")
        q_high_done, q_low_done = sem("q_high_done"), sem("q_low_done")
        lam_ready, lam_exp = sem("lam_ready"), sem("lam_exp")
        scores_full, exp_done, neg_m_ready, diff_ready = (sem(n) for n in ("scores_full", "exp_done", "neg_m_ready", "diff_ready"))
        dt_high_done, dt_low_done = sem("dt_high_done"), sem("dt_low_done")
        o_full, o_s_done, o_tok_done, ssq_done = (sem(n) for n in ("o_full", "o_s_done", "o_tok_done", "ssq_done"))
        rms_ready, rms_pow = sem("rms_ready"), sem("rms_pow")
        dve_chain = sem("dve_chain")

        xb = lambda b: x[:, b * BT:(b + 1) * BT, :]
        raw = lambda ap: ap.bitcast(F32)
        use_at = {}

        XT = (0, 1, 0)
        norm_no = lambda ph, b: ph * NB + b
        unit_no = lambda ph, u: (ph // 2) * NB * NU + u
        gated_no = lambda ph, u: (ph // 2) * NB * E + (u // NU) * E + min(u % NU, E)
        GATES = [(0, 0, NT)] + [(2, b * BT, BT) for b in range(NB)]
        gate_no = {(ph, t): i for i, (ph, t0, n) in enumerate(GATES) for t in range(t0, t0 + n)}

        def released(kind, *at):
            if kind == "xt":
                return xt_low_done, norm_no(*at) + 1
            if kind == "logits":
                return logits_read, gate_no[at] + 1
            if kind == "gates":
                return gates_t_done, (at[0] // 2) * NB + at[1] + 1
            if kind == "out":
                return ffn_added, (at[0] // 2) * NB + at[1] + 1
            if kind == "dt":
                return dt_low_done, NCH * at[0] + at[1] + 1
            done = {"a": a_low_done, "v": v_low_done, "q": q_low_done, "o": o_tok_done}[kind]
            return done, (at[0] if at else 0) + 1

        OUT_AT, LN_AT, V_AT = NU + LAG, NU + LAG + 1, NU + LAG + 3
        FFN_STEPS = NB * NU + V_AT - NU + 1

        def side(s):
            for kind, at in (("out", OUT_AT), ("norm", LN_AT), ("v", V_AT)):
                b, r = divmod(s - at, NU)
                if r == 0 and 0 <= b < NB:
                    yield kind, b

        def a_step(t):
            if t % 2 == 1 and t < NT - 1:
                yield "q", (t + 1) // 2
            if t % 2 == 1 and t >= 5:
                yield "o", (t - 5) // 2
            if t % 4 == 3 and t >= 7:
                yield "norm", (t - 7) // 4

        A_STEPS = NT + 4

        block = ctx.enter_context(nc.Block())

        @block.tensor
        def _(pe):
            def use(*name):
                if use_at:
                    pe.wait_ge(*released(*list(use_at)[-1]))
                use_at[name] = len(use_at)

            def three(o_ap, hi_lo_st, hi_lo_mv, start=True, stop=True):
                (sh, sl), (mh, ml) = hi_lo_st, hi_lo_mv
                nc.tensor.matmul(o_ap, sh, mh, start=start, stop=False)
                nc.tensor.matmul(o_ap, sl, mh, start=False, stop=False)
                return nc.tensor.matmul(o_ap, sh, ml, start=False, stop=stop)

            def turn_norm(ph, b):
                use("xt", ph, b)
                pe.wait_ge(xn_ready, norm_no(ph, b) + 1)
                for j in range(BT):
                    last = nc.tensor.transpose(turn[:, j * P:(j + 1) * P], xn[:, j, :], ident[:])
                last.then_inc(turn_full, 1)

            def wait_xt(ph, b):
                pe.wait_ge(xt_high_done, norm_no(ph, b) + 1)
                pe.wait_ge(xt_low_done, norm_no(ph, b) + 1)

            def xt_parts(ph, a, n):
                return xt_high[XT[ph]][:, a:a + n], xt_low[XT[ph]][:, a:a + n]

            def logits(ph, t0, n):
                use("logits", ph, t0)
                for t in range(t0, t0 + n):
                    if t % BT == 0:
                        wait_xt(ph, t // BT)
                    last = three(turn[:, (t - t0) * E:(t - t0 + 1) * E], xt_parts(ph, t * P, P),
                                 (gw_high[:], gw_low[:]))
                last.then_inc(turn_full, 1)

            def turn_gates(ph, t0, n):
                for b in range(t0 // BT, (t0 + n) // BT):
                    use("gates", ph, b)
                    pe.wait_ge(gate_rows_ready, gate_no[ph, t0] + 1)
                    for j in range(BT):
                        last = nc.tensor.transpose(turn[:, j * P:(j + 1) * P],
                                                   gate_rows[:, (b * BT + j) * GR:(b * BT + j) * GR + P], ident[:])
                    last.then_inc(turn_full, 1)

            pe.wait_ge(pool_const, 2)
            for b in range(NB):
                turn_norm(0, b)
            pe.wait_ge(gw_low_done, 1)
            logits(0, 0, NT)

            use("a")
            pe.wait_ge(aw_low_done, 1)
            for h in range(2):
                wq = (aw_high[:, h, :], aw_low[:, h, :])
                wk = (aw_high[:, 2 + h, :], aw_low[:, 2 + h, :])
                last = three(turn[:, h * P:(h + 1) * P], wq, wk)
            last.then_inc(turn_full, 1)
            turn_gates(0, 0, NT)

            def ffn(ph):
                for s in range(FFN_STEPS):
                    b, e = divmod(s, NU)
                    n = unit_no(ph, s)
                    if s < NB * NU:
                        mv_ = xt_parts(ph, b * BLK, BLK)
                        if ph == 0 and b == 0 and e % WCH == 0:
                            pe.wait_ge(w_low_done, e // WCH + 1)
                        if e == 0:
                            wait_xt(ph, b)
                            if ph == 2 and b == 0:
                                pe.wait_ge(exp_done, 4 * NT)
                        if n >= 2:
                            pe.wait_ge(silu_done, n - 1)
                        three(ps_h1(n), (w_high[:, e, 0, :], w_low[:, e, 0, :]), mv_).then_inc(h1_full, 1)
                        if n >= 2:
                            pe.wait_ge(prod_done, n - 1)
                        three(ps_h3(n), (w_high[:, e, 1, :], w_low[:, e, 1, :]), mv_).then_inc(h3_full, 1)
                        if e < E:
                            g = gated_no(ph, s)
                            if e == 0:
                                pe.wait_ge(gates_t_done, (ph // 2) * NB + b + 1)
                                pe.wait_ge(pool_const, 10)
                            if g:
                                pe.wait_ge(gated_done, g)
                            nc.tensor.matmul(single[:], pick[:, e, :],
                                             gates_t[:, b * BLK:(b + 1) * BLK],
                                             start=True, stop=True).then_inc(gb_full, 1)
                    r = s - LAG
                    if 0 <= r < NB * NU:
                        rb, re = divmod(r, NU)
                        rn = unit_no(ph, r)
                        if re == 0:
                            ob = (ph // 2) * NB + rb
                            if ob >= 2:
                                pe.wait_ge(out_s_done, ob - 1)
                        pe.wait_ge(h_high_done, rn + 1)
                        pe.wait_ge(h_low_done, rn + 1)
                        last = three(ps_out(rb), (w_high[:, re, 2, :], w_low[:, re, 2, :]),
                                     (h_high(rn), h_low(rn)), start=(re == 0), stop=False)
                        last.then_inc(second_done, 1)
                        if re == NU - 1:
                            nc.tensor.matmul(ps_out(rb), b2_st[:], gates_t[:, rb * BLK:(rb + 1) * BLK],
                                             start=False, stop=True).then_inc(out_full, 1)
                    for kind, b in side(s):
                        if kind == "out":
                            use("out", ph, b)
                            pe.wait_ge(out_s_done, (ph // 2) * NB + b + 1)
                            for j in range(BT):
                                last = nc.tensor.transpose(turn[:, j * P:(j + 1) * P],
                                                           out_s[:, j * P:(j + 1) * P], ident[:])
                            last.then_inc(turn_full, 1)
                        if kind == "norm" and ph == 0:
                            turn_norm(1, b)
                        if kind == "v" and ph == 0:
                            use("v", b)
                            wait_xt(1, b)
                            for j in range(BT):
                                last = three(turn[:, j * P:(j + 1) * P], xt_parts(1, (b * BT + j) * P, P),
                                             (aw_high[:, 4, :], aw_low[:, 4, :]))
                            last.then_inc(turn_full, 1)

            pe.wait_ge(b2_low_done, 1)
            ffn(0)

            def project_q(g):
                use("q", g)
                wait_xt(1, g // 2)
                pe.wait_ge(a_high_done, 1)
                pe.wait_ge(a_low_done, 1)
                for h in range(2):
                    last = three(turn[:, h * GRP:(h + 1) * GRP], (a_high[:, h, :], a_low[:, h, :]),
                                 xt_parts(1, g * GRP, GRP))
                last.then_inc(turn_full, 1)

            def scores(t, h, half):
                n = 4 * t + 2 * h + half
                if n >= 3:
                    pe.wait_ge(exp_done, n - 2)
                if h == 0 and half == 0 and t % GT_ == 0:
                    pe.wait_ge(q_high_done, t // GT_ + 1)
                    pe.wait_ge(q_low_done, t // GT_ + 1)
                g = (t // GT_) % 2
                a = h * GRP + (t % GT_) * P
                for c in range(2):
                    k = half * HALF + c * CH
                    last = three(slots[n % 3][:, c * CH:(c + 1) * CH],
                                 (q_high[:, g, a:a + P], q_low[:, g, a:a + P]), xt_parts(1, k, CH))
                last.then_inc(scores_full, 1)

            def turn_diff(t, c):
                if not 0 <= t < NT:
                    return
                use("dt", t, c)
                pe.wait_ge(diff_ready, 2 * t + c // 2 + 1)
                for j in range(4):
                    last = nc.tensor.transpose(turn[:, j * P:(j + 1) * P],
                                               p_rows[:, t % 2, (4 * c + j) * P:(4 * c + j + 1) * P], ident[:])
                last.then_inc(turn_full, 1)

            def times_v(g, piece):
                if not 0 <= g < NG:
                    return
                if piece == 0:
                    if g:
                        pe.wait_ge(o_s_done, g)
                    pe.wait_ge(dt_high_done, 4 * GT_ * (g + 1))
                    pe.wait_ge(dt_low_done, 4 * GT_ * (g + 1))
                for k in range(piece * NT // 2, (piece + 1) * NT // 2):
                    last = three(single[:, 0:GRP], (v_high[:, k, :], v_low[:, k, :]),
                                 (dt_parts[:, g % 2, 0, k, :], dt_parts[:, g % 2, 1, k, :]),
                                 start=(k == 0), stop=(k == NT - 1))
                if piece:
                    last.then_inc(o_full, 1)

            pe.wait_ge(v_high_done, NB)
            pe.wait_ge(v_low_done, NB)
            project_q(0)
            for t in range(A_STEPS):
                if t < NT:
                    scores(t, 0, 0)
                turn_diff(t - 2, 2)
                if t < NT:
                    scores(t, 0, 1)
                turn_diff(t - 2, 3)
                if t % 2 == 0:
                    times_v((t - 4) // 2, 1)
                if t < NT:
                    scores(t, 1, 0)
                turn_diff(t - 1, 0)
                if t < NT:
                    scores(t, 1, 1)
                turn_diff(t - 1, 1)
                if t % 2 == 1:
                    times_v((t - 3) // 2, 0)
                for kind, i in a_step(t):
                    if kind == "q":
                        project_q(i)
                    if kind == "o":
                        use("o", i)
                        pe.wait_ge(o_s_done, i + 1)
                        for j in range(GT_):
                            last = nc.tensor.transpose(turn[:, j * P:(j + 1) * P],
                                                       o_s[:, j * P:(j + 1) * P], ident[:])
                        last.then_inc(turn_full, 1)
                    if kind == "norm":
                        turn_norm(2, i)
                        logits(2, i * BT, BT)
                        turn_gates(2, i * BT, BT)
            ffn(2)

        def turned(eng, *name):
            eng.wait_ge(turn_full, use_at[name] + 1)

        @block.scalar
        def _(act):
            def copy(o_ap, i_ap, scale=1.0):
                return nc.scalar.activation(o_ap, i_ap, ACT.Copy, scale=scale)

            def norm_high(ph, b):
                turned(act, "xt", ph, b)
                copy(xt_high[XT[ph]][:, b * BLK:(b + 1) * BLK], turn[:]).then_inc(xt_high_done, 1)

            def gate_exp(ph, t0, n):
                act.wait_ge(z_ready, gate_no[ph, t0] + 1)
                nc.scalar.activation(ez[:, 0:n, :], z[:, 0:n, :], ACT.Exp).then_inc(ez_done, 1)

            def gates_copy(ph, t0, n):
                for b in range(t0 // BT, (t0 + n) // BT):
                    turned(act, "gates", ph, b)
                    copy(gates_t[0:GR, b * BLK:(b + 1) * BLK], turn[0:GR, :]).then_inc(gates_t_done, 1)

            act.wait_ge(cols_in_s, 16)
            copy(gw_high[:], cols[:, 2 * NU:2 * NU + E]).then_inc(gw_high_done, 1)
            for c in range(NWC):
                act.wait_ge(w_in_s[c], 16)
                copy(w_high[:, c * WCH:(c + 1) * WCH, :, :], w_raw[:, c * WCH:(c + 1) * WCH, :, :]).then_inc(w_high_done, 1)
            for b in range(NB):
                norm_high(0, b)
            act.wait_ge(aw_in_s, 16)
            copy(aw_high[:], aw_raw[:]).then_inc(aw_high_done, 1)
            act.wait_ge(b2_in_s, 32)
            act.wait_ge(pool_const, 6)
            copy(b2_st[0:BHI, :], b2_raw[0:BHI, :]).then_inc(b2_high_done, 1)
            copy(b2_high[LOW:LOW + BLO, :], b2_raw[LOW:LOW + BLO, :]).then_inc(b2_high_done, 1)
            act.wait_ge(lam_ready, 1)
            nc.scalar.activation(lam_e[:], lam_s[:], ACT.Exp).then_inc(lam_exp, 1)
            gate_exp(0, 0, NT)
            turned(act, "a")
            copy(a_high[:].rearrange("p h c -> p (h c)"), turn[:, 0:2 * P]).then_inc(a_high_done, 1)
            gates_copy(0, 0, NT)

            def ffn(ph):
                for s in range(FFN_STEPS):
                    n = unit_no(ph, s)
                    if s < NB * NU:
                        act.wait_ge(h1_full, n + 1)
                        if n >= 2:
                            act.wait_ge(prod_done, n - 1)
                        nc.scalar.activation(silu_s(n), ps_h1(n), ACT.Silu, bias=b1(s % NU)).then_inc(silu_done, 1)
                    r = s - 1
                    if 0 <= r < NB * NU:
                        rn = unit_no(ph, r)
                        act.wait_ge(prod_done, rn + 1)
                        act.wait_ge(gated_done, gated_no(ph, r) + (r % NU < E))
                        if rn >= HR:
                            act.wait_ge(second_done, rn - HR + 1)
                        copy(h_high(rn), gated(rn)).then_inc(h_high_done, 1)
                    for kind, b in side(s):
                        ob = (ph // 2) * NB + b
                        if kind == "out":
                            act.wait_ge(out_full, ob + 1)
                            if ob:
                                act.wait_ge(ffn_added, ob)
                            copy(out_s[:], ps_out(b), scale=0.5).then_inc(out_s_done, 1)
                        if kind == "norm" and ph == 0:
                            norm_high(1, b)
                        if kind == "v" and ph == 0:
                            turned(act, "v", b)
                            copy(v_high[:, b * BT:(b + 1) * BT, :], turn[:].rearrange("p (t d) -> p t d", t=BT)).then_inc(v_high_done, 1)

            ffn(0)

            def q_copy(g):
                turned(act, "q", g)
                copy(q_high[:, g % 2, :], turn[:]).then_inc(q_high_done, 1)

            def dt_copy(t, c):
                if not 0 <= t < NT:
                    return
                turned(act, "dt", t, c)
                q = (t % GT_) * P
                copy(dt_parts[:, (t // GT_) % 2, 0, 4 * c:4 * c + 4, q:q + P],
                     turn[:].rearrange("p (k q) -> p k q", k=4)).then_inc(dt_high_done, 1)

            def exps(t, h):
                act.wait_ge(neg_m_ready, 2 * t + h + 1)
                if h == 0 and t >= 2:
                    act.wait_ge(turn_full, use_at["dt", t - 2, 3] + 1)
                for half in range(2):
                    n = 4 * t + 2 * h + half
                    if h == 1 and t >= 1:
                        act.wait_ge(diff_ready, 2 * (t - 1) + half + 1)
                    nc.scalar.activation(p_rows[:, 2 if h else t % 2, half * HALF:(half + 1) * HALF],
                                         slots[n % 3][:], ACT.Exp, bias=neg_m[:, t % 2, h:h + 1], scale=SCALE,
                                         accum_out=sums[:, t % 2, h, half:half + 1]).then_inc(exp_done, 1)

            q_copy(0)
            for t in range(A_STEPS):
                dt_copy(t - 2, 2)
                dt_copy(t - 2, 3)
                if t < NT:
                    exps(t, 0)
                if t % 2 == 0 and 0 <= (t - 4) // 2 < NG:
                    act.wait_ge(o_full, (t - 4) // 2 + 1)
                    if t > 4:
                        act.wait_ge(ssq_done, GT_ * ((t - 4) // 2))
                    copy(o_s[:], single[:, 0:GRP]).then_inc(o_s_done, 1)
                dt_copy(t - 1, 0)
                dt_copy(t - 1, 1)
                if t < NT:
                    exps(t, 1)
                for kind, i in a_step(t):
                    if kind == "q":
                        q_copy(i)
                    if kind == "o":
                        turned(act, "o", i)
                        if i:
                            act.wait_ge(attn_added, i)
                        nc.scalar.activation(o_tok[:].rearrange("p t d -> p (t d)"), turn[:, 0:GRP], ACT.Copy).then_inc(o_tok_done, 1)
                        act.wait_ge(o_tok_done, i + 1)
                        for j in range(GT_):
                            if j:
                                act.wait_ge(ssq_done, GT_ * i + j)
                            nc.scalar.activation(o_s[:, 0:D], o_tok[:, j, :], ACT.Square,
                                                 accum_out=ssq[:, j:j + 1]).then_inc(ssq_done, 1)
                    if kind == "norm":
                        norm_high(2, i)
                        gate_exp(2, i * BT, BT)
                        gates_copy(2, i * BT, BT)
            ffn(2)

        @block.gpsimd
        def _(pool):
            nc.gpsimd.memset(ident[:], 0.0).then_inc(pool_const, 1)
            pool.wait_ge(pool_const, 1)
            nc.gpsimd.affine_select(out=ident[:], in_=ident[:], compare_op=ALU.not_equal, fill=1.0, base=0,
                                    pattern=[[-1, P]], channel_multiplier=1).then_inc(pool_const, 1)
            nc.gpsimd.memset(mhalf[:], -0.5).then_inc(pool_const, 1)
            for e in range(E):
                last = nc.gpsimd.memset(rank[:, e:e + 1], float(E - e))
            last.then_inc(pool_const, 1)
            nc.gpsimd.memset(gate_rows[:], 1.0).then_inc(pool_const, 1)
            nc.gpsimd.memset(raw(b2_st[:]), 0.0).then_inc(pool_const, 1)
            nc.gpsimd.memset(raw(gates_t[:]), 0.0).then_inc(pool_const, 1)
            nc.gpsimd.memset(raw(pick[:]), 0.0).then_inc(pool_const, 1)

            def to_minus_half(src, dst, ready, done, n):
                pool.wait_ge(ready, n)
                nc.gpsimd.tensor_tensor(dst, src, mhalf[:, 0:src.shape[1]], ALU.pow).then_inc(done, 1)

            def low(dst, src, high):
                return nc.gpsimd.tensor_tensor(dst, src, raw(high), ALU.subtract)

            pool.wait_ge(pool_const, 3)
            for b in range(NB):
                to_minus_half(ve[:], y0[:], ve_ready, pow_done, b + 1)
            pool.wait_ge(gw_high_done, 1)
            low(gw_low[:], cols[:, 2 * NU:2 * NU + E], gw_high[:]).then_inc(gw_low_done, 1)
            for i, first in enumerate((0, E)):
                pool.wait_ge(pool_const, 8 + i)
                nc.gpsimd.affine_select(out=pick[:], in_=raw(pick[:]), compare_op=ALU.not_equal, fill=1.0, base=-first,
                                        pattern=[[-1, E], [0, P]], channel_multiplier=1).then_inc(pool_const, 1)
            for c in range(NWC):
                pool.wait_ge(w_high_done, c + 1)
                u = slice(c * WCH, (c + 1) * WCH)
                low(w_low[:, u, :, :], w_raw[:, u, :, :], w_high[:, u, :, :]).then_inc(w_low_done, 1)
                if c == 0:
                    pool.wait_ge(aw_high_done, 1)
                    low(aw_low[:], aw_raw[:], aw_high[:]).then_inc(aw_low_done, 1)

            def ffn(ph):
                for s in range(FFN_STEPS):
                    r = s - 1
                    if 0 <= r < NB * NU:
                        rn = unit_no(ph, r)
                        pool.wait_ge(h_high_done, rn + 1)
                        nc.gpsimd.tensor_tensor(h_low(rn), gated(rn), raw(h_high(rn)), ALU.subtract).then_inc(h_low_done, 1)
                    for kind, b in side(s):
                        if kind == "out" and ph == 0:
                            to_minus_half(ve[:], y0[:], ve_ready, pow_done, norm_no(1, b) + 1)

            ffn(0)
            for t in range(A_STEPS):
                for kind, i in a_step(t):
                    if kind == "o":
                        to_minus_half(f1[:], f2[:], rms_ready, rms_pow, i + 1)
                    if kind == "norm":
                        to_minus_half(ve[:], y0[:], ve_ready, pow_done, norm_no(2, i) + 1)
            ffn(2)

        @block.vector
        def _(dve):
            n_chain = [0]

            def link(ins):
                n_chain[0] += 1
                ins.then_inc(dve_chain, 1)
                dve.wait_ge(dve_chain, n_chain[0])

            def newton(v, y, t, o_ap):
                link(nc.vector.tensor_tensor(t, y, y, ALU.mult))
                link(nc.vector.tensor_tensor(t, t, v, ALU.mult))
                link(nc.vector.tensor_scalar(t, t, -0.5, 1.5, ALU.mult, ALU.add))
                link(nc.vector.tensor_tensor(o_ap, y, t, ALU.mult))

            def row_norm(ph, b):
                k = norm_no(ph, b)
                if ph == 0:
                    dve.wait_ge(x_in_s[b], 16)
                for j in range(BT):
                    last = nc.vector.bn_stats(stats[:, j, :], x[:, b * BT + j, :])
                link(last)
                for j in range(BT):
                    last = nc.vector.bn_aggr(mv[:, j, :], stats[:, j, :])
                link(last)
                nc.vector.tensor_scalar(ve[:], mv[:, :, 1], EPS, None, ALU.add).then_inc(ve_ready, 1)
                dve.wait_ge(ve_ready, k + 1)
                dve.wait_ge(pow_done, k + 1)
                newton(ve[:], y0[:], ya[:], rstd[:])
                if k:
                    dve.wait_ge(turn_full, last_xt_use(ph, b) + 1)
                for j in range(BT):
                    last = nc.vector.tensor_scalar(xn[:, j, :], x[:, b * BT + j, :], mv[:, j, 0:1], rstd[:, j:j + 1],
                                                   ALU.subtract, ALU.mult)
                last.then_inc(xn_ready, 1)

            def last_xt_use(ph, b):
                return use_at["xt", ph, b - 1] if b else use_at["xt", ph - 1, NB - 1]

            def low(dst, src, high):
                return nc.vector.tensor_tensor(dst, src, raw(high), ALU.subtract)

            def norm_low(ph, b):
                tok = slice(b * BLK, (b + 1) * BLK)
                dve.wait_ge(xt_high_done, norm_no(ph, b) + 1)
                low(xt_low[XT[ph]][:, tok], turn[:], xt_high[XT[ph]][:, tok]).then_inc(xt_low_done, 1)

            def best(src, n, top, marks, sel):
                over = lambda ap: ap[:, 0:n].unsqueeze(2).to_broadcast([P, n, E])
                ranks = rank[:].unsqueeze(1).to_broadcast([P, n, E])
                link(nc.vector.tensor_reduce(top[:, 0:n], src, AX_X, ALU.max))
                link(nc.vector.tensor_tensor(marks, src, over(top), ALU.is_equal))
                link(nc.vector.tensor_tensor(marks, marks, ranks, ALU.mult))
                link(nc.vector.tensor_reduce(top[:, 0:n], marks, AX_X, ALU.max))
                link(nc.vector.tensor_tensor(sel, marks, over(top), ALU.is_equal))

            def gates(ph, t0, n):
                k = gate_no[ph, t0]
                over = lambda ap: ap[:, 0:n].unsqueeze(2).to_broadcast([P, n, E])
                z_, ez_, a, b, hi = (m[:, 0:n, :] for m in (z, ez, g1, g2, g_high))
                turned(dve, "logits", ph, t0)
                if k == 0:
                    dve.wait_ge(gb_in_s, 16)
                    dve.wait_ge(pool_const, 5)
                nc.vector.tensor_tensor(a, turn[:, 0:n * E].rearrange("p (t e) -> p t e", e=E),
                                        gb[:].unsqueeze(1).to_broadcast([P, n, E]), ALU.add).then_inc(logits_read, 1)
                dve.wait_ge(logits_read, k + 1)
                link(nc.vector.tensor_reduce(gs[:, 0:n], a, AX_X, ALU.max))
                nc.vector.tensor_tensor(z_, a, over(gs), ALU.subtract).then_inc(z_ready, 1)
                dve.wait_ge(z_ready, k + 1)
                dve.wait_ge(ez_done, k + 1)
                link(nc.vector.tensor_reduce(gs[:, 0:n], ez_, AX_X, ALU.add))
                link(nc.vector.reciprocal(gs[:, 0:n], gs[:, 0:n]))
                link(nc.vector.tensor_tensor(a, ez_, over(gs), ALU.mult))
                best(a, n, gs, b, b)
                link(nc.vector.scalar_tensor_tensor(ez_, b, -2.0, a, ALU.mult, ALU.add))
                best(ez_, n, gs, z_, z_)
                link(nc.vector.tensor_tensor(b, b, z_, ALU.add))
                link(nc.vector.tensor_tensor(a, a, b, ALU.mult))
                link(nc.vector.tensor_copy(hi, a))
                rows = gate_rows[:, t0 * GR:(t0 + n) * GR].rearrange("p (t r) -> p t r", r=GR)
                nc.vector.tensor_copy(rows[:, :, 0:E], raw(hi))
                nc.vector.tensor_copy(rows[:, :, LOW:LOW + E], raw(hi))
                nc.vector.tensor_tensor(rows[:, :, E:2 * E], a, raw(hi), ALU.subtract).then_inc(gate_rows_ready, 1)

            for b in range(NB):
                row_norm(0, b)
                norm_low(0, b)
            dve.wait_ge(lam_in_s, 16)
            link(nc.vector.tensor_tensor(lam_prod[:], lam_in[:, 0:4:2, :], lam_in[:, 1:4:2, :], ALU.mult))
            nc.vector.tensor_reduce(lam_s[:], lam_prod[:], AX_X, ALU.add).then_inc(lam_ready, 1)
            gates(0, 0, NT)
            dve.wait_ge(b2_high_done, 2)
            low(b2_st[LOW:LOW + BLO, :], b2_raw[LOW:LOW + BLO, :], b2_high[LOW:LOW + BLO, :]).then_inc(b2_low_done, 1)
            dve.wait_ge(lam_exp, 1)
            link(nc.vector.tensor_tensor(neg_lam[:], lam_e[:, 1:2], lam_e[:, 0:1], ALU.subtract))
            link(nc.vector.tensor_scalar(neg_lam[:], neg_lam[:], -LAMBDA_INIT, None, ALU.add))
            dve.wait_ge(a_high_done, 1)
            low(a_low[:].rearrange("p h c -> p (h c)"), turn[:, 0:2 * P],
                a_high[:].rearrange("p h c -> p (h c)")).then_inc(a_low_done, 1)

            def ffn(ph):
                for s in range(FFN_STEPS):
                    n = unit_no(ph, s)
                    if s < NB * NU:
                        e = s % NU
                        g = gated_no(ph, s)
                        dve.wait_ge(h3_full, n + 1)
                        dve.wait_ge(silu_done, n + 1)
                        if e >= E and n >= WR:
                            dve.wait_ge(h_low_done, n - WR + 1)
                        nc.vector.scalar_tensor_tensor(prod_s(n) if e < E else gated(n), ps_h3(n), b3(e), silu_s(n),
                                                       ALU.add, ALU.mult).then_inc(prod_done, 1)
                        if e < E:
                            dve.wait_ge(prod_done, n + 1)
                            dve.wait_ge(gb_full, g + 1)
                            if n >= WR:
                                dve.wait_ge(h_low_done, n - WR + 1)
                            nc.vector.tensor_tensor(gated(n), single[:], prod_s(n), ALU.mult).then_inc(gated_done, 1)
                    for kind, b in side(s):
                        if kind == "out":
                            turned(dve, "out", ph, b)
                            flat = xb(b).rearrange("p t d -> p (t d)")
                            nc.vector.tensor_tensor(flat, turn[:], flat, ALU.add).then_inc(ffn_added, 1)
                            if ph == 0:
                                dve.wait_ge(ffn_added, b + 1)
                                row_norm(1, b)
                        if kind == "norm" and ph == 0:
                            norm_low(1, b)
                        if kind == "v" and ph == 0:
                            dve.wait_ge(v_high_done, b + 1)
                            low(v_low[:, b * BT:(b + 1) * BT, :], turn[:].rearrange("p (t d) -> p t d", t=BT),
                                v_high[:, b * BT:(b + 1) * BT, :]).then_inc(v_low_done, 1)

            ffn(0)

            def q_low_part(g):
                dve.wait_ge(q_high_done, g + 1)
                low(q_low[:, g % 2, :], turn[:], q_high[:, g % 2, :]).then_inc(q_low_done, 1)

            def dt_low_part(t, c):
                if not 0 <= t < NT:
                    return
                q = slice((t % GT_) * P, (t % GT_ + 1) * P)
                g = (t // GT_) % 2
                dve.wait_ge(dt_high_done, NCH * t + c + 1)
                low(dt_parts[:, g, 1, 4 * c:4 * c + 4, q], turn[:].rearrange("p (k q) -> p k q", k=4),
                    dt_parts[:, g, 0, 4 * c:4 * c + 4, q]).then_inc(dt_low_done, 1)

            def row_max(t, h, half):
                n = 4 * t + 2 * h + half
                dve.wait_ge(scores_full, n + 1)
                if half == 0 and 2 * t + h >= 2:
                    dve.wait_ge(neg_m_ready, 2 * t + h - 1)
                link(nc.vector.tensor_reduce(maxes[:, h, half:half + 1], slots[n % 3][:], AX_X, ALU.max))
                if half:
                    nc.vector.tensor_scalar(neg_m[:, t % 2, h:h + 1], maxes[:, h, 0:1], maxes[:, h, 1:2], -SCALE,
                                            ALU.max, ALU.mult).then_inc(neg_m_ready, 1)

            def combine(t):
                if not 0 <= t < NT:
                    return
                i = t % 2
                dve.wait_ge(exp_done, 4 * (t + 1))
                link(nc.vector.tensor_tensor(total[:], sums[:, i, :, 0], sums[:, i, :, 1], ALU.add))
                nc.vector.reciprocal(r1[:, t:t + 1], total[:, 0:1])
                link(nc.vector.reciprocal(r2[:], total[:, 1:2]))
                link(nc.vector.tensor_scalar(neg_c[:], total[:, 0:1], r2[:], neg_lam[:], ALU.mult, ALU.mult))
                for half in range(2):
                    k = slice(half * HALF, (half + 1) * HALF)
                    nc.vector.scalar_tensor_tensor(p_rows[:, i, k], p_rows[:, 2, k], neg_c[:], p_rows[:, i, k],
                                                   ALU.mult, ALU.add).then_inc(diff_ready, 1)

            def add_attention(g):
                r = r1[:, g * GT_:(g + 1) * GT_]
                dve.wait_ge(ssq_done, GT_ * (g + 1))
                link(nc.vector.tensor_tensor(f1[:], r, r, ALU.mult))
                link(nc.vector.tensor_tensor(f1[:], f1[:], ssq[:], ALU.mult))
                nc.vector.tensor_scalar(f1[:], f1[:], 1.0 / D, EPS, ALU.mult, ALU.add).then_inc(rms_ready, 1)
                dve.wait_ge(rms_ready, g + 1)
                dve.wait_ge(rms_pow, g + 1)
                newton(f1[:], f2[:], ya[:, 0:GT_], f3[:])
                link(nc.vector.scalar_tensor_tensor(f3[:], f3[:], 1.0 - LAMBDA_INIT, r, ALU.mult, ALU.mult))
                dve.wait_ge(o_tok_done, g + 1)
                for j in range(GT_):
                    xj = x[:, g * GT_ + j, :]
                    last = nc.vector.scalar_tensor_tensor(xj, o_tok[:, j, :], f3[:, j:j + 1], xj, ALU.mult, ALU.add)
                last.then_inc(attn_added, 1)

            q_low_part(0)
            for t in range(A_STEPS):
                if t < NT:
                    row_max(t, 0, 0)
                dt_low_part(t - 2, 2)
                if t < NT:
                    row_max(t, 0, 1)
                dt_low_part(t - 2, 3)
                combine(t - 1)
                if t < NT:
                    row_max(t, 1, 0)
                dt_low_part(t - 1, 0)
                if t < NT:
                    row_max(t, 1, 1)
                dt_low_part(t - 1, 1)
                for kind, i in a_step(t):
                    if kind == "q":
                        q_low_part(i)
                    if kind == "o":
                        add_attention(i)
                    if kind == "norm":
                        dve.wait_ge(attn_added, 2 * i + 2)
                        row_norm(2, i)
                        norm_low(2, i)
                        gates(2, i * BT, BT)
            ffn(2)

        @block.sync
        def _(sp):
            x_rows = x_in.rearrange("(t p) d -> p t d", p=P)
            out_rows = out.rearrange("(t p) d -> p t d", p=P)
            w_rows = w_units.rearrange("p (u k c) -> p u k c", k=3, c=P)
            for b in range(NB):
                sp.dma_start(xb(b), x_rows[:, b * BT:(b + 1) * BT, :]).then_inc(x_in_s[b], 16)
                if b == 0:
                    sp.dma_start(cols[:], cols_in).then_inc(cols_in_s, 16)
            for c in range(NWC):
                sp.dma_start(w_raw[:, c * WCH:(c + 1) * WCH, :, :], w_rows[:, c * WCH:(c + 1) * WCH, :, :]).then_inc(w_in_s[c], 16)
                if c == 0:
                    sp.dma_start(aw_raw[:], attn_w.rearrange("p (k c) -> p k c", c=P)).then_inc(aw_in_s, 16)
                    sp.dma_start(gb[:], gate_b[0, :].partition_broadcast(P)).then_inc(gb_in_s, 16)
                    sp.dma_start(lam_in[:], lambdas.partition_broadcast(P)).then_inc(lam_in_s, 16)
                    sp.dma_start(b2_raw[0:BHI, :], b2_rows[0:BHI, :]).then_inc(b2_in_s, 16)
                    sp.dma_start(b2_raw[LOW:LOW + BLO, :], b2_rows[BHI:BHI + BLO, :]).then_inc(b2_in_s, 16)
            for b in range(NB):
                sp.wait_ge(ffn_added, NB + b + 1)
                sp.dma_start(out_rows[:, b * BT:(b + 1) * BT, :], xb(b)).then_inc(out_stored, 16)
            sp.wait_ge(out_stored, 16 * NB)


def kernel(L0_attn_x, L0_attn_w_q12, L0_attn_w_k12, L0_attn_w_v, L0_attn_lambda_q1, L0_attn_lambda_k1,
           L0_attn_lambda_q2, L0_attn_lambda_k2, L0_ffn_gate_w, L0_ffn_gate_b, L0_ffn_w1, L0_ffn_b1, L0_ffn_w3,
           L0_ffn_b3, L0_ffn_w2, L0_ffn_b2, L0_ffn_ws1, L0_ffn_bs1, L0_ffn_ws3, L0_ffn_bs3, L0_ffn_ws2, L0_ffn_bs2):
    import numpy as np
    import concourse.bacc as bacc
    from concourse.bass_utils import run_bass_kernel_spmd

    B, T, D = L0_attn_x.shape
    S = L0_ffn_ws1.shape[0] // P
    as_np = lambda a: np.asarray(a)
    first = np.concatenate([as_np(L0_ffn_w1), as_np(L0_ffn_ws1).reshape(S, P, D)]).transpose(2, 0, 1)
    third = np.concatenate([as_np(L0_ffn_w3), as_np(L0_ffn_ws3).reshape(S, P, D)]).transpose(2, 0, 1)
    second = np.concatenate([as_np(L0_ffn_w2), as_np(L0_ffn_ws2).reshape(D, S, P).transpose(1, 0, 2)]).transpose(2, 0, 1)
    w_units = np.stack([first, third, second], axis=2).reshape(P, -1)
    b1 = np.concatenate([as_np(L0_ffn_b1), as_np(L0_ffn_bs1).reshape(S, P)]).T
    b3 = np.concatenate([as_np(L0_ffn_b3), as_np(L0_ffn_bs3).reshape(S, P)]).T
    cols = np.concatenate([b1, b3, as_np(L0_ffn_gate_w).T], axis=1)
    b2, bs2 = as_np(L0_ffn_b2), as_np(L0_ffn_bs2)[None, :]
    b2_rows = np.concatenate([b2, b2, bs2, b2, bs2])
    wq, wk = as_np(L0_attn_w_q12), as_np(L0_attn_w_k12)
    attn_w = np.concatenate([wq[:, 0:D].T, wq[:, D:2 * D].T, wk[:, 0:D].T, wk[:, D:2 * D].T, as_np(L0_attn_w_v)], axis=1)
    lambdas = np.stack([as_np(a) for a in (L0_attn_lambda_q1, L0_attn_lambda_k1, L0_attn_lambda_q2, L0_attn_lambda_k2)])
    ins = {"x_in": as_np(L0_attn_x).reshape(T, D), "w_units": w_units, "cols_in": cols,
           "gate_b": as_np(L0_ffn_gate_b)[None, :], "b2_rows": b2_rows, "attn_w": attn_w, "lambdas": lambdas}
    ins = {k: np.ascontiguousarray(a) for k, a in ins.items()}

    nc = bacc.Bacc("TRN2", target_bir_lowering=False, num_devices=1)
    args = [nc.dram_tensor(k, a.shape, mybir.dt.from_np(a.dtype), kind="ExternalInput").ap() for k, a in ins.items()]
    result = nc.dram_tensor("result", (T, D), F32, kind="ExternalOutput").ap()
    macaron(nc, *args, result)
    r = run_bass_kernel_spmd(nc, [ins], core_ids=[0])
    return r.results[0]["result"].reshape(B, T, D)
```

```python
from contextlib import ExitStack

import concourse.bass as bass
from concourse import mybir
from concourse.alu_op_type import AluOpType as ALU

F32 = mybir.dt.float32
F32R = mybir.dt.float32r
ACT = mybir.ActivationFunctionType
AX_X = mybir.AxisListType.X

P = 128
TOP = 2


def macaron(nc, x_in, w_units, cols_in, gate_b, b2_rows, attn_w, lambdas, out):
    T, D = x_in.shape
    E = gate_b.shape[1]
    NT = T // P
    BT = 4
    BLK = BT * P
    NB = NT // BT
    NU = w_units.shape[1] // (3 * P)
    NSH = NU - E
    GT_ = 2
    GRP = GT_ * P
    NG = NT // GT_
    CH = BLK
    NCH = T // CH
    HALF = T // 2
    assert D == P and T == NB * BLK and NCH == 4 and NB * 2 == NG
    SCALE = float(D) ** -0.25
    EPS = 1e-5
    LAMBDA_INIT = 0.8
    LAG = 3
    HR = 4
    WR = 3
    WCH = 2
    NWC = NU // WCH
    ONE, LOW = 2 * E, 32
    GR = LOW + E + 1
    BHI, BLO = 2 * E + 1, E + 1

    with ExitStack() as ctx:
        def sb(name, shape, dt=F32):
            return ctx.enter_context(nc.sbuf_tensor(name, shape, dt))

        def sem(name):
            return ctx.enter_context(nc.semaphore(name))

        WORD = 4
        ARENA = (5 * 2 * BT * GRP + (2 * HR + WR + 1) * BLK + 3 * T) * WORD
        ARENA0 = (nc.sbuf_base + 31) // 32 * 32
        sb("arena", [P, ARENA // WORD + 8])

        x = sb("x", [P, NT, D])
        xt_high = [sb(f"xt_high{i}", [P, T], F32R) for i in range(2)]
        xt_low = [sb(f"xt_low{i}", [P, T], F32R) for i in range(2)]
        w_high = sb("w_high", [P, NU, 3, P], F32R)
        w_low = sb("w_low", [P, NU, 3, P], F32R)
        v_high = sb("v_high", [P, NT, D], F32R)
        v_low = sb("v_low", [P, NT, D], F32R)
        gates_t = sb("gates_t", [P, T], F32R)
        gate_rows = sb("gate_rows", [P, (NT - 1) * GR + P])
        pick = sb("pick", [P, E, P], F32R)
        q_high = sb("q_high", [P, 2, 2 * GRP], F32R)
        q_low = sb("q_low", [P, 2, 2 * GRP], F32R)
        a_high = sb("a_high", [P, 2, P], F32R)
        a_low = sb("a_low", [P, 2, P], F32R)
        b2_st = sb("b2_st", [P, P], F32R)
        gw_high = sb("gw_high", [P, E], F32R)
        gw_low = sb("gw_low", [P, E], F32R)
        ident = sb("ident", [P, P])
        cols = sb("cols", [P, 2 * NU + E])
        b1 = lambda u: cols[:, u:u + 1]
        b3 = lambda u: cols[:, NU + u:NU + u + 1]
        gb = sb("gb", [P, E])
        rank = sb("rank", [P, E])
        mhalf = sb("mhalf", [P, BT])
        stats = sb("stats", [P, BT, 6])
        mv = sb("mv", [P, BT, 2])
        ve, y0, ya, rstd = (sb(n, [P, BT]) for n in ("ve", "y0", "ya", "rstd"))
        xn = sb("xn", [P, BT, D])
        z, ez, g1, g2 = (sb(n, [P, NT, E]) for n in ("z", "ez", "g1", "g2"))
        g_high = sb("g_high", [P, NT, E], F32R)
        gs = sb("gs", [P, NT])
        lam_s, lam_e = sb("lam_s", [P, 2]), sb("lam_e", [P, 2])
        neg_lam = sb("neg_lam", [P, 1])
        o_s = sb("o_s", [P, GRP])
        o_tok = sb("o_tok", [P, GT_, D])
        ssq, f1, f2, f3, ft = (sb(n, [P, GT_]) for n in ("ssq", "f1", "f2", "f3", "ft"))
        maxes = sb("maxes", [P, 2, 2])
        neg_m = sb("neg_m", [P, 2, 2])
        sums = sb("sums", [P, 2, 2, 2])
        total = sb("total", [P, 2])
        r2 = sb("r2", [P, 1])
        r1 = sb("r1", [P, NT])
        neg_c = sb("neg_c", [P, 2])


        def at(name, shape, word, dt=F32):
            size = 1
            for k in shape[1:]:
                size *= k
            assert (word + size) * WORD <= ARENA
            return nc.alloc_sbuf_tensor_at(name, shape, dt, offset=ARENA0 + word * WORD), word + size

        dt_parts, w = at("dt_parts", [P, 5, 2, BT, GRP], 0, F32R)
        h_ring, w = at("h_ring", [P, HR, 2, BLK], w, F32R)
        gated_ring, w = at("gated_ring", [P, WR, BLK], w)
        out_s, w = at("out_s", [P, BLK], w)
        p_rows, _ = at("p_rows", [P, 3, T], w)
        silu_ring, w = at("silu_ring", [P, 2, BLK], w)
        prod_ring, w = at("prod_ring", [P, 2, BLK], w)
        w_raw, w = at("w_raw", [P, NU, 3, P], 0)
        aw_raw, w = at("aw_raw", [P, 5, P], w)
        aw_high, w = at("aw_high", [P, 5, P], w, F32R)
        aw_low, w = at("aw_low", [P, 5, P], w, F32R)
        b2_raw, w = at("b2_raw", [P, P], w)
        b2_high, w = at("b2_high", [P, P], w, F32R)
        lam_in, w = at("lam_in", [P, 4, D], w)
        lam_prod, w = at("lam_prod", [P, 2, D], w)
        assert w <= 5 * 2 * BT * GRP
        h_high = lambda u: h_ring[:, u % HR, 0, :]
        h_low = lambda u: h_ring[:, u % HR, 1, :]
        silu_s = lambda u: silu_ring[:, u % 2, :]
        prod_s = lambda u: prod_ring[:, u % 2, :]
        gated = lambda u: gated_ring[:, u % WR, :]

        slots = [ctx.enter_context(nc.psum_tensor(f"slot{i}", [P, 2 * BLK], F32)) for i in range(2)]
        bank = {i: ctx.enter_context(nc.psum_tensor(f"bank{i}", [P, BLK], F32)) for i in range(4, 8)}
        single = bank[7]
        ps_h1 = lambda u: slots[0][:, (u % 2) * BLK:(u % 2 + 1) * BLK]
        ps_h3 = lambda u: slots[1][:, (u % 2) * BLK:(u % 2 + 1) * BLK]
        out_bank = lambda b: 4 + b % 2
        gate_bank = lambda ph, b: 5 if (ph, b) == (2, 0) else 7
        FFN_TURN, SIDE_TURN = 6, 5
        dt_bank = lambda c: 4 + 2 * (c % 2)
        dt_chunk = lambda g, c: NCH if c == NCH - 1 and g % 2 else c

        x_in_s = [sem(f"x_in{b}") for b in range(NB)]
        w_in_s = [sem(f"w_in{c}") for c in range(NWC)]
        aw_in_s, cols_in_s, gb_in_s, b2_in_s, lam_in_s = (sem(n) for n in ("aw_in", "cols_in", "gb_in", "b2_in", "lam_in_s"))
        out_stored = sem("out_stored")
        pool_const = sem("pool_const")
        w_high_done, w_low_done = sem("w_high_done"), sem("w_low_done")
        gw_high_done, gw_low_done = sem("gw_high_done"), sem("gw_low_done")
        aw_high_done, aw_low_done = sem("aw_high_done"), sem("aw_low_done")
        b2_high_done, b2_low_done = sem("b2_high_done"), sem("b2_low_done")
        turn_full, logits_read = sem("turn_full"), sem("logits_read")
        ve_ready, pow_done, xn_ready = sem("ve_ready"), sem("pow_done"), sem("xn_ready")
        xt_high_done, xt_low_done = sem("xt_high_done"), sem("xt_low_done")
        z_ready, ez_done, gate_rows_ready, gates_t_done = (sem(n) for n in ("z_ready", "ez_done", "gate_rows_ready", "gates_t_done"))
        h1_full, h3_full, gb_full = sem("h1_full"), sem("h3_full"), sem("gb_full")
        silu_done, prod_done, gated_done = sem("silu_done"), sem("prod_done"), sem("gated_done")
        h_high_done, h_low_done, second_done = sem("h_high_done"), sem("h_low_done"), sem("second_done")
        out_full, out_s_done = sem("out_full"), sem("out_s_done")
        ffn_added, attn_added = sem("ffn_added"), sem("attn_added")
        a_high_done, a_low_done = sem("a_high_done"), sem("a_low_done")
        v_high_done, v_low_done = sem("v_high_done"), sem("v_low_done")
        q_high_done, q_low_done = sem("q_high_done"), sem("q_low_done")
        lam_ready, lam_exp = sem("lam_ready"), sem("lam_exp")
        scores_full, exp_done, neg_m_ready = (sem(n) for n in ("scores_full", "exp_done", "neg_m_ready"))
        neg_c_ready, scaled_done, diff0_ready, diff1_ready = (sem(n) for n in ("neg_c_ready", "scaled_done", "diff0_ready", "diff1_ready"))
        dt_high_done, dt_low_done = sem("dt_high_done"), sem("dt_low_done")
        o_full, o_s_done, o_tok_done, ssq_done = (sem(n) for n in ("o_full", "o_s_done", "o_tok_done", "ssq_done"))
        rms_ready, rms_pow = sem("rms_ready"), sem("rms_pow")
        dve_chain, cleared = sem("dve_chain"), sem("cleared")

        xb = lambda b: x[:, b * BT:(b + 1) * BT, :]
        raw = lambda ap: ap.bitcast(F32)
        use_at = {}

        XT = (0, 1, 0)
        norm_no = lambda ph, b: ph * NB + b
        unit_no = lambda ph, u: (ph // 2) * NB * NU + u
        gated_no = lambda ph, u: (ph // 2) * NB * E + (u // NU) * E + max(u % NU - NSH, 0)
        BATCHES = [(0, 0, BT), (0, BT, BT), (0, 2 * BT, 2 * BT), (2, 0, 2 * BT), (2, 2 * BT, 2 * BT)]
        STAGES = 20
        logits_no = lambda ph, b: (ph // 2) * NB + b

        def released(kind, *at):
            if kind == "xt":
                return xt_low_done, norm_no(*at) + 1
            if kind == "logits":
                return logits_read, logits_no(*at) + 1
            if kind == "gates":
                return gates_t_done, (at[0] // 2) * NB + at[1] + 1
            if kind == "out":
                return ffn_added, (at[0] // 2) * NB + at[1] + 1
            if kind == "dt":
                return dt_low_done, NCH * at[0] + at[1] + 1
            done = {"a": a_low_done, "v": v_low_done, "q": q_low_done, "o": o_tok_done}[kind]
            return done, (at[0] if at else 0) + 1

        def attention_side(t, f):
            if (t, f) == (0, 0):
                yield "v", NB - 1
            if t % 2 == 1 and f == 0 and (t + 1) // 2 < NG:
                yield "q", (t + 1) // 2
            g, r = divmod(2 * t + f - 9, 4)
            for kind, at in (("o", 0), ("add_a", 1), ("add_b", 2)):
                gg = g if r == at else -1
                if 0 <= gg < NG:
                    yield kind, gg
            b, r = divmod(2 * t + f - 15, 8)
            for kind, at in (("norm_a", 0), ("norm_b", 1), ("xt", 2), ("logits", 3)):
                if r == at and 0 <= b < NB:
                    yield kind, 2, b
            first = 2 * t + f - 27
            if first == 0:
                yield "stages", 3, 0, 2
                yield "exp", 3
            if 1 <= first <= 4:
                yield "stages", 3, (2, 6, 10, 15)[first - 1], (6, 10, 15, STAGES)[first - 1]
            if first == 4:
                yield "gates", 2, 0
                yield "gates", 2, 1

        def side(ph, s):
            if ph == 0:
                for k, lo, hi, at in ((0, 2, 10, 0), (0, 10, STAGES, 1), (1, 2, 7, 6), (1, 7, 12, 7),
                                      (1, 12, 17, 8), (1, 17, STAGES, 9), (2, 2, 5, 11), (2, 5, 8, 12),
                                      (2, 8, 11, 13), (2, 11, 14, 14), (2, 14, 17, 15), (2, 17, STAGES, 16)):
                    if s == at:
                        yield "stages", k, lo, hi
                if s in (1, 3, 5):
                    yield "weights", (s + 3) // 2
                if s == 4:
                    yield "lambda_sums",
                if s == 12:
                    yield "attention_weights",
                if s == 20:
                    yield "a",
                for kind, at in (("norm_a", 0), ("norm_b", 1), ("xt", 2), ("logits", 3)):
                    bb, rr = divmod(s - at, 2)
                    if rr == 0 and 1 <= bb < NB:
                        yield kind, 0, bb
                for k, at in ((1, 5), (2, 10)):
                    if s == at:
                        yield "stages", k, 0, 2
                        yield "exp", k
                for b, at in enumerate((1, 9, 17, 18)):
                    if s == at:
                        yield "gates", 0, b
            if ph == 2:
                if 1 <= s <= 11:
                    t, f = divmod(2 * NT + s - 1, 2)
                    yield "attention", t, f
                if s == 12:
                    yield "stages", 4, 0, 2
                    yield "exp", 4
                if 13 <= s <= 18:
                    yield "stages", 4, 3 * (s - 13) + 2, 3 * (s - 13) + 5
                if s in (19, 20):
                    yield "gates", 2, s - 17
            for kind, at in (("out", 0), ("norm_a", 1), ("norm_b", 2), ("xt", 3)):
                b, r = divmod(s - NU - LAG - at, NU)
                if r == 0 and 0 <= b < NB and (at == 0 or ph == 0):
                    yield (kind, ph, b) if at == 0 else (kind, 1, b)
            if ph == 0:
                if s in (40, 41, 44):
                    yield "v", (40, 41, 44).index(s)
                if s == 42:
                    yield "q", 0

        FFN_STEPS = {0: NB * NU + LAG + 3, 2: NB * NU + LAG + 1}

        block = ctx.enter_context(nc.Block())

        @block.tensor
        def _(pe):
            last_use = {}

            def bank_free(i):
                if i in last_use:
                    pe.wait_ge(*released(*last_use[i]))

            def use(i, *name):
                bank_free(i)
                use_at[name] = len(use_at), i
                last_use[i] = name
                return bank[i]

            def three(o_ap, stationary, moving, start=True, stop=True):
                (sh, sl), (mh, ml) = stationary, moving
                nc.tensor.matmul(o_ap, sh, mh, start=start, stop=False)
                nc.tensor.matmul(o_ap, sl, mh, start=False, stop=False)
                return nc.tensor.matmul(o_ap, sh, ml, start=False, stop=stop)

            def turn(ps, src, n):
                for j in range(n):
                    last = nc.tensor.transpose(ps[:, j * P:(j + 1) * P], src(j), ident[:])
                last.then_inc(turn_full, 1)

            def wait_xt(ph, b):
                pe.wait_ge(xt_high_done, norm_no(ph, b) + 1)
                pe.wait_ge(xt_low_done, norm_no(ph, b) + 1)

            def xt_parts(ph, a, n):
                return xt_high[XT[ph]][:, a:a + n], xt_low[XT[ph]][:, a:a + n]

            def side_work(i, kind, *at):
                if kind == "xt":
                    ps = use(i, "xt", *at)
                    pe.wait_ge(xn_ready, norm_no(*at) + 1)
                    turn(ps, lambda j: xn[:, j, :], BT)
                if kind == "logits":
                    ph, b = at
                    ps = use(i, "logits", *at)
                    wait_xt(ph, b)
                    for j in range(BT):
                        last = three(ps[:, j * E:(j + 1) * E], xt_parts(ph, (b * BT + j) * P, P), (gw_high[:], gw_low[:]))
                    last.then_inc(turn_full, 1)
                if kind == "gates":
                    ph, b = at
                    ps = use(i, "gates", *at)
                    k = [k for k, (p, t0, n) in enumerate(BATCHES) if p == ph and t0 <= b * BT < t0 + n][0]
                    pe.wait_ge(gate_rows_ready, k + 1)
                    turn(ps, lambda j: gate_rows[:, (b * BT + j) * GR:(b * BT + j) * GR + P], BT)
                if kind == "out":
                    ps = use(i, "out", *at)
                    pe.wait_ge(out_s_done, (at[0] // 2) * NB + at[1] + 1)
                    turn(ps, lambda j: out_s[:, j * P:(j + 1) * P], BT)
                if kind == "a":
                    ps = use(i, "a")
                    pe.wait_ge(aw_low_done, 1)
                    for h in range(2):
                        last = three(ps[:, h * P:(h + 1) * P], (aw_high[:, h, :], aw_low[:, h, :]),
                                     (aw_high[:, 2 + h, :], aw_low[:, 2 + h, :]))
                    last.then_inc(turn_full, 1)
                if kind == "v":
                    b, = at
                    ps = use(i, "v", b)
                    wait_xt(1, b)
                    for j in range(BT):
                        last = three(ps[:, j * P:(j + 1) * P], xt_parts(1, (b * BT + j) * P, P),
                                     (aw_high[:, 4, :], aw_low[:, 4, :]))
                    last.then_inc(turn_full, 1)
                if kind == "q":
                    g, = at
                    ps = use(i, "q", g)
                    wait_xt(1, g // 2)
                    pe.wait_ge(a_low_done, 1)
                    for h in range(2):
                        last = three(ps[:, h * GRP:(h + 1) * GRP], (a_high[:, h, :], a_low[:, h, :]),
                                     xt_parts(1, g * GRP, GRP))
                    last.then_inc(turn_full, 1)
                if kind == "o":
                    g, = at
                    ps = use(i, "o", g)
                    turn(ps, lambda j: o_s[:, j * P:(j + 1) * P], GT_)
                if kind == "attention":
                    attention_half(i, *at)

            def ffn(ph):
                for s in range(FFN_STEPS[ph]):
                    b, e = divmod(s, NU)
                    n = unit_no(ph, s)
                    if s < NB * NU:
                        xt_block = xt_parts(ph, b * BLK, BLK)
                        if ph == 0 and b == 0 and e % WCH == 0:
                            pe.wait_ge(w_low_done, e // WCH + 1)
                        if e == 0:
                            wait_xt(ph, b)
                        if ph == 2 and s < 2:
                            pe.wait_ge(exp_done, 4 * NT - 1)
                        elif n >= 2:
                            pe.wait_ge(silu_done, n - 1)
                        three(ps_h1(n), (w_high[:, e, 0, :], w_low[:, e, 0, :]), xt_block).then_inc(h1_full, 1)
                        if ph == 2 and s < 2:
                            pe.wait_ge(exp_done, 4 * NT)
                        elif n >= 2:
                            pe.wait_ge(prod_done, n - 1)
                        three(ps_h3(n), (w_high[:, e, 1, :], w_low[:, e, 1, :]), xt_block).then_inc(h3_full, 1)
                        if e >= NSH:
                            g = gated_no(ph, s)
                            i = gate_bank(ph, b)
                            if e == NSH:
                                pe.wait_ge(gates_t_done, (ph // 2) * NB + b + 1)
                                bank_free(i)
                            if (ph, b, e) == (0, 0, NSH):
                                pe.wait_ge(pool_const, 7)
                            if (ph, b, e) == (2, 1, NSH):
                                pe.wait_ge(o_s_done, NG)
                            if g:
                                pe.wait_ge(gated_done, g)
                            nc.tensor.matmul(bank[i][:], pick[:, e - NSH, :], gates_t[:, b * BLK:(b + 1) * BLK],
                                             start=True, stop=True).then_inc(gb_full, 1)
                    r = s - LAG
                    if 0 <= r < NB * NU:
                        rb, re = divmod(r, NU)
                        rn = unit_no(ph, r)
                        ps = bank[out_bank(rb)]
                        if re == 0:
                            ob = (ph // 2) * NB + rb
                            if (ph, rb) == (2, 0):
                                bank_free(out_bank(0))
                            elif (ph, rb) == (2, 1):
                                pe.wait_ge(gated_done, gated_no(2, NU))
                            elif ob >= 2:
                                pe.wait_ge(out_s_done, ob - 1)
                        pe.wait_ge(h_high_done, rn + 1)
                        pe.wait_ge(h_low_done, rn + 1)
                        three(ps[:], (w_high[:, re, 2, :], w_low[:, re, 2, :]), (h_high(rn), h_low(rn)),
                              start=(re == 0), stop=False).then_inc(second_done, 1)
                        if re == NU - 1:
                            if (ph, rb) == (0, 0):
                                pe.wait_ge(b2_low_done, 1)
                            nc.tensor.matmul(ps[:], b2_st[:], gates_t[:, rb * BLK:(rb + 1) * BLK],
                                             start=False, stop=True).then_inc(out_full, 1)
                    for work in side(ph, s):
                        side_work(FFN_TURN, *work)

            def scores(t, h):
                for half in range(2):
                    n = 4 * t + 2 * h + half
                    if n >= 2:
                        pe.wait_ge(exp_done, n - 1)
                    if h == 0 and half == 0 and t % GT_ == 0:
                        pe.wait_ge(q_high_done, t // GT_ + 1)
                        pe.wait_ge(q_low_done, t // GT_ + 1)
                    if n == 1:
                        side_work(FFN_TURN, "xt", 1, NB - 1)
                        wait_xt(1, NB - 1)
                    g = (t // GT_) % 2
                    a = h * GRP + (t % GT_) * P
                    for c in range(2):
                        k = half * HALF + c * CH
                        last = three(slots[half][:, c * CH:(c + 1) * CH],
                                     (q_high[:, g, a:a + P], q_low[:, g, a:a + P]), xt_parts(1, k, CH))
                    last.then_inc(scores_full, 1)

            def times_v(g, c):
                if c == 0:
                    if g:
                        pe.wait_ge(o_s_done, g)
                    if g == 0:
                        pe.wait_ge(v_high_done, NB)
                        pe.wait_ge(v_low_done, NB)
                pe.wait_ge(dt_high_done, NCH * (GT_ * g + 1) + c + 1)
                pe.wait_ge(dt_low_done, NCH * (GT_ * g + 1) + c + 1)
                for j in range(BT):
                    k = BT * c + j
                    last = three(single[:, 0:GRP], (v_high[:, k, :], v_low[:, k, :]),
                                 (dt_parts[:, dt_chunk(g, c), 0, j, :], dt_parts[:, dt_chunk(g, c), 1, j, :]),
                                 start=(k == 0), stop=(k == NT - 1))
                if c == NCH - 1:
                    last.then_inc(o_full, 1)

            def attention_half(i, t, f):
                g, c = divmod(2 * t + f - 5, NCH)
                if 0 <= g < NG:
                    times_v(g, c)
                if 1 <= t <= NT:
                    for c in (2 * f, 2 * f + 1):
                        ps = use(dt_bank(c), "dt", t - 1, c)
                        if f == 0:
                            pe.wait_ge(diff0_ready, t)
                        else:
                            pe.wait_ge(diff1_ready, t)
                        turn(ps, lambda j: p_rows[:, (t - 1) % 2, (BT * c + j) * P:(BT * c + j + 1) * P], BT)
                for work in attention_side(t, f):
                    if work[0] == "o":
                        pe.wait_ge(o_s_done, work[1] + 1)
                    side_work(i, *work)

            pe.wait_ge(pool_const, 2)
            side_work(FFN_TURN, "xt", 0, 0)
            pe.wait_ge(gw_low_done, 1)
            side_work(FFN_TURN, "logits", 0, 0)
            ffn(0)
            for t in range(NT):
                for f in range(2):
                    scores(t, f)
                    attention_half(SIDE_TURN, t, f)
            ffn(2)

        def turned(eng, *name):
            k, i = use_at[name]
            eng.wait_ge(turn_full, k + 1)
            return bank[i]

        @block.scalar
        def _(act):
            def copy(o_ap, i_ap, scale=1.0):
                return nc.scalar.activation(o_ap, i_ap, ACT.Copy, scale=scale)

            def weights(c):
                act.wait_ge(w_in_s[c], 16)
                copy(w_high[:, c * WCH:(c + 1) * WCH, :, :], w_raw[:, c * WCH:(c + 1) * WCH, :, :]).then_inc(w_high_done, 1)

            def side_work(kind, *at):
                if kind == "weights":
                    weights(*at)
                if kind == "attention_weights":
                    act.wait_ge(aw_in_s, 16)
                    copy(aw_high[:], aw_raw[:]).then_inc(aw_high_done, 1)
                if kind == "xt":
                    ph, b = at
                    ps = turned(act, "xt", ph, b)
                    copy(xt_high[XT[ph]][:, b * BLK:(b + 1) * BLK], ps[:]).then_inc(xt_high_done, 1)
                if kind == "exp":
                    k, = at
                    _, t0, n = BATCHES[k]
                    act.wait_ge(z_ready, k + 1)
                    nc.scalar.activation(ez[:, t0:t0 + n, :], z[:, t0:t0 + n, :], ACT.Exp).then_inc(ez_done, 1)
                    if k == 1:
                        act.wait_ge(lam_ready, 1)
                        nc.scalar.activation(lam_e[:], lam_s[:], ACT.Exp).then_inc(lam_exp, 1)
                if kind == "gates":
                    ph, b = at
                    ps = turned(act, "gates", ph, b)
                    if (ph, b) == (0, 0):
                        act.wait_ge(cleared, 2)
                    copy(gates_t[0:GR, b * BLK:(b + 1) * BLK], ps[0:GR, :]).then_inc(gates_t_done, 1)
                if kind == "a":
                    ps = turned(act, "a")
                    copy(a_high[:].rearrange("p h c -> p (h c)"), ps[:, 0:2 * P]).then_inc(a_high_done, 1)
                if kind == "out":
                    ph, b = at
                    ob = (ph // 2) * NB + b
                    act.wait_ge(out_full, ob + 1)
                    if ob:
                        act.wait_ge(ffn_added, ob)
                    copy(out_s[:], bank[out_bank(b)][:], scale=0.5).then_inc(out_s_done, 1)
                if kind == "v":
                    b, = at
                    ps = turned(act, "v", b)
                    copy(v_high[:, b * BT:(b + 1) * BT, :], ps[:].rearrange("p (t d) -> p t d", t=BT)).then_inc(v_high_done, 1)
                if kind == "q":
                    g, = at
                    ps = turned(act, "q", g)
                    copy(q_high[:, g % 2, :], ps[:]).then_inc(q_high_done, 1)
                if kind == "o":
                    g, = at
                    ps = turned(act, "o", g)
                    if g:
                        act.wait_ge(attn_added, g)
                    copy(o_tok[:].rearrange("p t d -> p (t d)"), ps[:, 0:GRP]).then_inc(o_tok_done, 1)
                    act.wait_ge(o_tok_done, g + 1)
                    for j in range(GT_):
                        if j:
                            act.wait_ge(ssq_done, GT_ * g + j)
                        nc.scalar.activation(o_s[:, 0:D], o_tok[:, j, :], ACT.Square,
                                             accum_out=ssq[:, j:j + 1]).then_inc(ssq_done, 1)
                if kind == "attention":
                    attention_half(*at)

            def ffn(ph):
                for s in range(FFN_STEPS[ph]):
                    n = unit_no(ph, s)
                    if s < NB * NU:
                        act.wait_ge(h1_full, n + 1)
                        if n >= 2:
                            act.wait_ge(prod_done, n - 1)
                        if (ph, s) == (2, 0):
                            act.wait_ge(turn_full, use_at["dt", NT - 2, NCH - 1][0] + 1)
                        nc.scalar.activation(silu_s(n), ps_h1(n), ACT.Silu, bias=b1(s % NU)).then_inc(silu_done, 1)
                    r = s - 1
                    if 0 <= r < NB * NU:
                        rn = unit_no(ph, r)
                        if r % NU < NSH:
                            act.wait_ge(prod_done, rn + 1)
                        else:
                            act.wait_ge(gated_done, gated_no(ph, r) + 1)
                        if rn >= HR:
                            act.wait_ge(second_done, rn - HR + 1)
                        copy(h_high(rn), gated(rn)).then_inc(h_high_done, 1)
                    for work in side(ph, s):
                        side_work(*work)

            def dt_copy(t, c):
                if not 0 <= t < NT:
                    return
                ps = turned(act, "dt", t, c)
                q = slice((t % GT_) * P, (t % GT_ + 1) * P)
                copy(dt_parts[:, dt_chunk(t // GT_, c), 0, :, q], ps[:].rearrange("p (k q) -> p k q", k=BT)).then_inc(dt_high_done, 1)

            def exp(t, h, half):
                if t >= NT:
                    return
                if half == 0:
                    act.wait_ge(neg_m_ready, 2 * t + h + 1)
                    if h == 0 and t >= 2:
                        act.wait_ge(turn_full, use_at["dt", t - 2, NCH - 1][0] + 1)
                if h == 1 and t >= 1:
                    act.wait_ge((diff0_ready, diff1_ready)[half], t)
                nc.scalar.activation(p_rows[:, 2 if h else t % 2, half * HALF:(half + 1) * HALF], slots[half][:],
                                     ACT.Exp, bias=neg_m[:, t % 2, h:h + 1], scale=SCALE,
                                     accum_out=sums[:, t % 2, h, half:half + 1]).then_inc(exp_done, 1)

            def attention_half(t, f):
                if f == 0 and 1 <= t <= NT:
                    act.wait_ge(neg_c_ready, t)
                    act.wait_ge(exp_done, 4 * t)
                    copy(p_rows[:, 2, HALF:T], p_rows[:, 2, HALF:T], scale=neg_c[:, (t - 1) % 2:(t - 1) % 2 + 1]).then_inc(scaled_done, 1)
                dt_copy(t - 1, 2 * f)
                exp(t, f, 0)
                dt_copy(t - 1, 2 * f + 1)
                exp(t, f, 1)
                g, c = divmod(2 * t + f - 5, NCH)
                if 0 <= g < NG and c == NCH - 1:
                    act.wait_ge(o_full, g + 1)
                    if g:
                        act.wait_ge(ssq_done, GT_ * g)
                    copy(o_s[:], single[:, 0:GRP]).then_inc(o_s_done, 1)
                for work in attention_side(t, f):
                    side_work(*work)

            act.wait_ge(cols_in_s, 16)
            copy(gw_high[:], cols[:, 2 * NU:2 * NU + E]).then_inc(gw_high_done, 1)
            weights(0)
            weights(1)
            act.wait_ge(b2_in_s, 32)
            act.wait_ge(pool_const, 5)
            copy(b2_st[0:BHI, :], b2_raw[0:BHI, :]).then_inc(b2_high_done, 1)
            copy(b2_high[LOW:LOW + BLO, :], b2_raw[LOW:LOW + BLO, :]).then_inc(b2_high_done, 1)
            side_work("xt", 0, 0)
            side_work("exp", 0)
            ffn(0)
            side_work("xt", 1, NB - 1)
            for t in range(NT):
                for f in range(2):
                    attention_half(t, f)
            ffn(2)

        @block.gpsimd
        def _(pool):
            nc.gpsimd.memset(ident[:], 0.0).then_inc(pool_const, 1)
            pool.wait_ge(pool_const, 1)
            nc.gpsimd.affine_select(out=ident[:], in_=ident[:], compare_op=ALU.not_equal, fill=1.0, base=0,
                                    pattern=[[-1, P]], channel_multiplier=1).then_inc(pool_const, 1)
            nc.gpsimd.memset(mhalf[:], -0.5).then_inc(pool_const, 1)
            nc.gpsimd.memset(gate_rows[:], 1.0).then_inc(pool_const, 1)
            nc.gpsimd.memset(raw(b2_st[:]), 0.0).then_inc(pool_const, 1)
            pool.wait_ge(cleared, 1)
            for i, first in enumerate((0, E)):
                if i:
                    pool.wait_ge(pool_const, 6)
                nc.gpsimd.affine_select(out=pick[:], in_=raw(pick[:]), compare_op=ALU.not_equal, fill=1.0, base=-first,
                                        pattern=[[-1, E], [0, P]], channel_multiplier=1).then_inc(pool_const, 1)

            def to_minus_half(src, dst, ready, done, n):
                pool.wait_ge(ready, n)
                nc.gpsimd.tensor_tensor(dst, src, mhalf[:, 0:src.shape[1]], ALU.pow).then_inc(done, 1)

            def low(dst, src, high):
                return nc.gpsimd.tensor_tensor(dst, src, raw(high), ALU.subtract)

            def weights(c):
                pool.wait_ge(w_high_done, c + 1)
                u = slice(c * WCH, (c + 1) * WCH)
                low(w_low[:, u, :, :], w_raw[:, u, :, :], w_high[:, u, :, :]).then_inc(w_low_done, 1)

            def side_work(kind, *at):
                if kind == "norm_a":
                    to_minus_half(ve[:], y0[:], ve_ready, pow_done, norm_no(*at) + 1)
                if kind == "add_a":
                    to_minus_half(f1[:], f2[:], rms_ready, rms_pow, at[0] + 1)
                if kind == "weights":
                    weights(*at)
                if kind == "attention_weights":
                    pool.wait_ge(aw_high_done, 1)
                    low(aw_low[:], aw_raw[:], aw_high[:]).then_inc(aw_low_done, 1)
                if kind == "attention":
                    attention_half(*at)

            def attention_half(t, f):
                if f == 0 and 1 <= t <= NT:
                    pool.wait_ge(scaled_done, t)
                    p1 = p_rows[:, (t - 1) % 2, HALF:T]
                    nc.gpsimd.tensor_tensor(p1, p1, p_rows[:, 2, HALF:T], ALU.add).then_inc(diff1_ready, 1)
                for work in attention_side(t, f):
                    side_work(*work)

            def ffn(ph):
                for s in range(FFN_STEPS[ph]):
                    r = s - 1
                    if 0 <= r < NB * NU:
                        rn = unit_no(ph, r)
                        pool.wait_ge(h_high_done, rn + 1)
                        low(h_low(rn), gated(rn), h_high(rn)).then_inc(h_low_done, 1)
                    for work in side(ph, s):
                        side_work(*work)

            pool.wait_ge(pool_const, 3)
            side_work("norm_a", 0, 0)
            pool.wait_ge(gw_high_done, 1)
            low(gw_low[:], cols[:, 2 * NU:2 * NU + E], gw_high[:]).then_inc(gw_low_done, 1)
            weights(0)
            weights(1)
            ffn(0)
            for t in range(NT):
                for f in range(2):
                    attention_half(t, f)
            ffn(2)

        @block.vector
        def _(dve):
            count = [0]
            last_of = {}

            def did(chain, ins):
                count[0] += 1
                ins.then_inc(dve_chain, 1)
                last_of[chain] = count[0]

            def after(chain):
                dve.wait_ge(dve_chain, last_of[chain])

            def newton(chain, v, y, t, o_ap):
                did(chain, nc.vector.tensor_tensor(t, y, y, ALU.mult))
                after(chain)
                did(chain, nc.vector.tensor_tensor(t, t, v, ALU.mult))
                after(chain)
                did(chain, nc.vector.tensor_scalar(t, t, -0.5, 1.5, ALU.mult, ALU.add))
                after(chain)
                did(chain, nc.vector.tensor_tensor(o_ap, y, t, ALU.mult))

            def low(dst, src, high):
                return nc.vector.tensor_tensor(dst, src, raw(high), ALU.subtract)

            def best(part, src, top, marks, sel):
                n = src.shape[1]
                over = top.unsqueeze(2).to_broadcast([P, n, E])
                ranks = rank[:].unsqueeze(1).to_broadcast([P, n, E])
                if part == 0:
                    return nc.vector.tensor_reduce(top, src, AX_X, ALU.max)
                if part == 1:
                    return nc.vector.tensor_tensor(marks, src, over, ALU.is_equal)
                if part == 2:
                    return nc.vector.tensor_tensor(marks, marks, ranks, ALU.mult)
                if part == 3:
                    return nc.vector.tensor_reduce(top, marks, AX_X, ALU.max)
                return nc.vector.tensor_tensor(sel, marks, over, ALU.is_equal)

            def gate_stage(k, i):
                ph, t0, n = BATCHES[k]
                a, b, z_, ez_, hi = (m[:, t0:t0 + n, :] for m in (g1, g2, z, ez, g_high))
                top = gs[:, t0:t0 + n]
                over = top.unsqueeze(2).to_broadcast([P, n, E])
                if i == 0:
                    dve.wait_ge(logits_read, logits_no(ph, (t0 + n) // BT - 1) + 1)
                    did("gate", nc.vector.tensor_reduce(top, a, AX_X, ALU.max))
                    return
                after("gate")
                if i == 1:
                    nc.vector.tensor_tensor(z_, a, over, ALU.subtract).then_inc(z_ready, 1)
                    return
                if i == 2:
                    dve.wait_ge(z_ready, k + 1)
                    dve.wait_ge(ez_done, k + 1)
                    did("gate", nc.vector.tensor_reduce(top, ez_, AX_X, ALU.add))
                if i == 3:
                    did("gate", nc.vector.reciprocal(top, top))
                if i == 4:
                    did("gate", nc.vector.tensor_tensor(a, ez_, over, ALU.mult))
                if 5 <= i < 10:
                    did("gate", best(i - 5, a, top, b, b))
                if i == 10:
                    did("gate", nc.vector.scalar_tensor_tensor(ez_, b, -2.0, a, ALU.mult, ALU.add))
                if 11 <= i < 16:
                    did("gate", best(i - 11, ez_, top, z_, z_))
                if i == 16:
                    did("gate", nc.vector.tensor_tensor(b, b, z_, ALU.add))
                if i == 17:
                    did("gate", nc.vector.tensor_tensor(a, a, b, ALU.mult))
                if i == 18:
                    did("gate", nc.vector.tensor_copy(hi, a))
                if i == 19:
                    rows = gate_rows[:, t0 * GR:(t0 + n) * GR].rearrange("p (t r) -> p t r", r=GR)
                    nc.vector.tensor_copy(rows[:, :, 0:E], raw(hi))
                    nc.vector.tensor_copy(rows[:, :, LOW:LOW + E], raw(hi))
                    nc.vector.tensor_tensor(rows[:, :, E:2 * E], a, raw(hi), ALU.subtract).then_inc(gate_rows_ready, 1)

            def side_work(kind, *at):
                if kind == "norm_a":
                    ph, b = at
                    if ph == 0:
                        dve.wait_ge(x_in_s[b], 16)
                    if ph == 1:
                        dve.wait_ge(ffn_added, b + 1)
                    if ph == 2:
                        dve.wait_ge(attn_added, 2 * (b + 1))
                    for j in range(BT):
                        last = nc.vector.bn_stats(stats[:, j, :], x[:, b * BT + j, :])
                    did("norm", last)
                    after("norm")
                    for j in range(BT):
                        last = nc.vector.bn_aggr(mv[:, j, :], stats[:, j, :])
                    did("norm", last)
                    after("norm")
                    nc.vector.tensor_scalar(ve[:], mv[:, :, 1], EPS, None, ALU.add).then_inc(ve_ready, 1)
                if kind == "norm_b":
                    ph, b = at
                    k = norm_no(ph, b)
                    dve.wait_ge(ve_ready, k + 1)
                    dve.wait_ge(pow_done, k + 1)
                    newton("norm", ve[:], y0[:], ya[:], rstd[:])
                    after("norm")
                    if k:
                        dve.wait_ge(xt_high_done, k)
                    for j in range(BT):
                        last = nc.vector.tensor_scalar(xn[:, j, :], x[:, b * BT + j, :], mv[:, j, 0:1], rstd[:, j:j + 1],
                                                       ALU.subtract, ALU.mult)
                    last.then_inc(xn_ready, 1)
                if kind == "xt":
                    ph, b = at
                    tok = slice(b * BLK, (b + 1) * BLK)
                    ps = turned(dve, "xt", ph, b)
                    dve.wait_ge(xt_high_done, norm_no(ph, b) + 1)
                    low(xt_low[XT[ph]][:, tok], ps[:], xt_high[XT[ph]][:, tok]).then_inc(xt_low_done, 1)
                if kind == "logits":
                    ph, b = at
                    ps = turned(dve, "logits", ph, b)
                    if (ph, b) == (0, 0):
                        dve.wait_ge(gb_in_s, 16)
                    nc.vector.tensor_tensor(g1[:, b * BT:(b + 1) * BT, :], ps[:, 0:BT * E].rearrange("p (t e) -> p t e", e=E),
                                            gb[:].unsqueeze(1).to_broadcast([P, BT, E]), ALU.add).then_inc(logits_read, 1)
                if kind == "stages":
                    k, lo, hi = at
                    if (k, lo) == (0, 2):
                        dve.wait_ge(pool_const, 4)
                    for i in range(lo, hi):
                        gate_stage(k, i)
                if kind == "lambda_sums":
                    dve.wait_ge(lam_in_s, 16)
                    did("lambda", nc.vector.tensor_tensor(lam_prod[:], lam_in[:, 0:4:2, :], lam_in[:, 1:4:2, :], ALU.mult))
                    after("lambda")
                    nc.vector.tensor_reduce(lam_s[:], lam_prod[:], AX_X, ALU.add).then_inc(lam_ready, 1)
                if kind == "a":
                    dve.wait_ge(lam_exp, 1)
                    did("lambda", nc.vector.tensor_tensor(neg_lam[:], lam_e[:, 1:2], lam_e[:, 0:1], ALU.subtract))
                    after("lambda")
                    did("lambda", nc.vector.tensor_scalar(neg_lam[:], neg_lam[:], -LAMBDA_INIT, None, ALU.add))
                    ps = turned(dve, "a")
                    dve.wait_ge(a_high_done, 1)
                    low(a_low[:].rearrange("p h c -> p (h c)"), ps[:, 0:2 * P],
                        a_high[:].rearrange("p h c -> p (h c)")).then_inc(a_low_done, 1)
                if kind == "out":
                    ph, b = at
                    ps = turned(dve, "out", ph, b)
                    flat = xb(b).rearrange("p t d -> p (t d)")
                    nc.vector.tensor_tensor(flat, ps[:], flat, ALU.add).then_inc(ffn_added, 1)
                if kind == "v":
                    b, = at
                    ps = turned(dve, "v", b)
                    dve.wait_ge(v_high_done, b + 1)
                    low(v_low[:, b * BT:(b + 1) * BT, :], ps[:].rearrange("p (t d) -> p t d", t=BT),
                        v_high[:, b * BT:(b + 1) * BT, :]).then_inc(v_low_done, 1)
                if kind == "q":
                    g, = at
                    ps = turned(dve, "q", g)
                    dve.wait_ge(q_high_done, g + 1)
                    low(q_low[:, g % 2, :], ps[:], q_high[:, g % 2, :]).then_inc(q_low_done, 1)
                if kind == "add_a":
                    g, = at
                    r = r1[:, g * GT_:(g + 1) * GT_]
                    dve.wait_ge(ssq_done, GT_ * (g + 1))
                    did("add", nc.vector.tensor_tensor(f1[:], r, r, ALU.mult))
                    after("add")
                    did("add", nc.vector.tensor_tensor(f1[:], f1[:], ssq[:], ALU.mult))
                    after("add")
                    nc.vector.tensor_scalar(f1[:], f1[:], 1.0 / D, EPS, ALU.mult, ALU.add).then_inc(rms_ready, 1)
                if kind == "add_b":
                    g, = at
                    r = r1[:, g * GT_:(g + 1) * GT_]
                    dve.wait_ge(rms_ready, g + 1)
                    dve.wait_ge(rms_pow, g + 1)
                    newton("add", f1[:], f2[:], ft[:], f3[:])
                    after("add")
                    did("add", nc.vector.scalar_tensor_tensor(f3[:], f3[:], 1.0 - LAMBDA_INIT, r, ALU.mult, ALU.mult))
                    after("add")
                    dve.wait_ge(o_tok_done, g + 1)
                    for j in range(GT_):
                        xj = x[:, g * GT_ + j, :]
                        last = nc.vector.scalar_tensor_tensor(xj, o_tok[:, j, :], f3[:, j:j + 1], xj, ALU.mult, ALU.add)
                    last.then_inc(attn_added, 1)
                if kind == "attention":
                    attention_half(*at)

            def ffn(ph):
                for s in range(FFN_STEPS[ph]):
                    n = unit_no(ph, s)
                    if s < NB * NU:
                        b, e = divmod(s, NU)
                        g = gated_no(ph, s)
                        dve.wait_ge(h3_full, n + 1)
                        dve.wait_ge(silu_done, n + 1)
                        if e < NSH and n >= WR:
                            dve.wait_ge(h_low_done, n - WR + 1)
                        nc.vector.scalar_tensor_tensor(gated(n) if e < NSH else prod_s(n), ps_h3(n), b3(e), silu_s(n),
                                                       ALU.add, ALU.mult).then_inc(prod_done, 1)
                        if e >= NSH:
                            dve.wait_ge(prod_done, n + 1)
                            dve.wait_ge(gb_full, g + 1)
                            if n >= WR:
                                dve.wait_ge(h_low_done, n - WR + 1)
                            nc.vector.tensor_tensor(gated(n), bank[gate_bank(ph, b)][:], prod_s(n), ALU.mult).then_inc(gated_done, 1)
                    for work in side(ph, s):
                        side_work(*work)

            def dt_low_part(t, c):
                if not 0 <= t < NT:
                    return
                q = slice((t % GT_) * P, (t % GT_ + 1) * P)
                k = dt_chunk(t // GT_, c)
                ps = turned(dve, "dt", t, c)
                dve.wait_ge(dt_high_done, NCH * t + c + 1)
                low(dt_parts[:, k, 1, :, q], ps[:].rearrange("p (k q) -> p k q", k=BT),
                    dt_parts[:, k, 0, :, q]).then_inc(dt_low_done, 1)

            def row_max(t, h):
                if t >= NT:
                    return
                if 2 * t + h >= 2:
                    dve.wait_ge(neg_m_ready, 2 * t + h - 1)
                for half in range(2):
                    dve.wait_ge(scores_full, 4 * t + 2 * h + half + 1)
                    did("max", nc.vector.tensor_reduce(maxes[:, h, half:half + 1], slots[half][:], AX_X, ALU.max))
                after("max")
                nc.vector.tensor_scalar(neg_m[:, t % 2, h:h + 1], maxes[:, h, 0:1], maxes[:, h, 1:2], -SCALE,
                                        ALU.max, ALU.mult).then_inc(neg_m_ready, 1)

            def combine(t):
                i = t % 2
                dve.wait_ge(exp_done, 4 * (t + 1))
                did("combine", nc.vector.tensor_tensor(total[:], sums[:, i, :, 0], sums[:, i, :, 1], ALU.add))
                after("combine")
                did("combine", nc.vector.reciprocal(r2[:], total[:, 1:2]))
                did("add", nc.vector.reciprocal(r1[:, t:t + 1], total[:, 0:1]))
                after("combine")
                nc.vector.tensor_scalar(neg_c[:, i:i + 1], total[:, 0:1], r2[:], neg_lam[:], ALU.mult, ALU.mult).then_inc(neg_c_ready, 1)
                dve.wait_ge(neg_c_ready, t + 1)
                nc.vector.scalar_tensor_tensor(p_rows[:, i, 0:HALF], p_rows[:, 2, 0:HALF], neg_c[:, i:i + 1],
                                               p_rows[:, i, 0:HALF], ALU.mult, ALU.add).then_inc(diff0_ready, 1)

            def attention_half(t, f):
                if f == 0 and 1 <= t <= NT:
                    combine(t - 1)
                row_max(t, f)
                dt_low_part(t - 1, 2 * f)
                dt_low_part(t - 1, 2 * f + 1)
                for work in attention_side(t, f):
                    side_work(*work)

            nc.vector.memset(raw(pick[:]), 0.0).then_inc(cleared, 1)
            nc.vector.memset(raw(gates_t[:]), 0.0).then_inc(cleared, 1)
            for e in range(E):
                last = nc.vector.memset(rank[:, e:e + 1], float(E - e))
            did("gate", last)
            side_work("norm_a", 0, 0)
            side_work("norm_b", 0, 0)
            side_work("xt", 0, 0)
            dve.wait_ge(b2_high_done, 2)
            low(b2_st[LOW:LOW + BLO, :], b2_raw[LOW:LOW + BLO, :], b2_high[LOW:LOW + BLO, :]).then_inc(b2_low_done, 1)
            side_work("logits", 0, 0)
            side_work("stages", 0, 0, 2)
            ffn(0)
            side_work("xt", 1, NB - 1)
            for t in range(NT):
                for f in range(2):
                    attention_half(t, f)
            ffn(2)

        @block.sync
        def _(sp):
            x_rows = x_in.rearrange("(t p) d -> p t d", p=P)
            out_rows = out.rearrange("(t p) d -> p t d", p=P)
            w_rows = w_units.rearrange("p (u k c) -> p u k c", k=3, c=P)
            load_x = lambda b: sp.dma_start(xb(b), x_rows[:, b * BT:(b + 1) * BT, :]).then_inc(x_in_s[b], 16)

            def load_weights(c):
                sp.dma_start(w_raw[:, c * WCH:(c + 1) * WCH, :, :], w_rows[:, c * WCH:(c + 1) * WCH, :, :]).then_inc(w_in_s[c], 16)

            load_x(0)
            sp.dma_start(cols[:], cols_in).then_inc(cols_in_s, 16)
            load_weights(0)
            sp.dma_start(gb[:], gate_b[0, :].partition_broadcast(P)).then_inc(gb_in_s, 16)
            load_weights(1)
            sp.dma_start(b2_raw[0:BHI, :], b2_rows[0:BHI, :]).then_inc(b2_in_s, 16)
            sp.dma_start(b2_raw[LOW:LOW + BLO, :], b2_rows[BHI:BHI + BLO, :]).then_inc(b2_in_s, 16)
            for b in range(1, NB):
                load_x(b)
            for c in range(2, NWC):
                load_weights(c)
            sp.dma_start(lam_in[:], lambdas.partition_broadcast(P)).then_inc(lam_in_s, 16)
            sp.dma_start(aw_raw[:], attn_w.rearrange("p (k c) -> p k c", c=P)).then_inc(aw_in_s, 16)
            for b in range(NB):
                sp.wait_ge(ffn_added, NB + b + 1)
                sp.dma_start(out_rows[:, b * BT:(b + 1) * BT, :], xb(b)).then_inc(out_stored, 16)
            sp.wait_ge(out_stored, 16 * NB)


def kernel(L0_attn_x, L0_attn_w_q12, L0_attn_w_k12, L0_attn_w_v, L0_attn_lambda_q1, L0_attn_lambda_k1,
           L0_attn_lambda_q2, L0_attn_lambda_k2, L0_ffn_gate_w, L0_ffn_gate_b, L0_ffn_w1, L0_ffn_b1, L0_ffn_w3,
           L0_ffn_b3, L0_ffn_w2, L0_ffn_b2, L0_ffn_ws1, L0_ffn_bs1, L0_ffn_ws3, L0_ffn_bs3, L0_ffn_ws2, L0_ffn_bs2):
    import numpy as np
    import concourse.bacc as bacc
    from concourse.bass_utils import run_bass_kernel_spmd

    B, T, D = L0_attn_x.shape
    S = L0_ffn_ws1.shape[0] // P
    as_np = lambda a: np.asarray(a)
    first = np.concatenate([as_np(L0_ffn_ws1).reshape(S, P, D), as_np(L0_ffn_w1)]).transpose(2, 0, 1)
    third = np.concatenate([as_np(L0_ffn_ws3).reshape(S, P, D), as_np(L0_ffn_w3)]).transpose(2, 0, 1)
    second = np.concatenate([as_np(L0_ffn_ws2).reshape(D, S, P).transpose(1, 0, 2), as_np(L0_ffn_w2)]).transpose(2, 0, 1)
    w_units = np.stack([first, third, second], axis=2).reshape(P, -1)
    b1 = np.concatenate([as_np(L0_ffn_bs1).reshape(S, P), as_np(L0_ffn_b1)]).T
    b3 = np.concatenate([as_np(L0_ffn_bs3).reshape(S, P), as_np(L0_ffn_b3)]).T
    cols = np.concatenate([b1, b3, as_np(L0_ffn_gate_w).T], axis=1)
    b2, bs2 = as_np(L0_ffn_b2), as_np(L0_ffn_bs2)[None, :]
    b2_rows = np.concatenate([b2, b2, bs2, b2, bs2])
    wq, wk = as_np(L0_attn_w_q12), as_np(L0_attn_w_k12)
    attn_w = np.concatenate([wq[:, 0:D].T, wq[:, D:2 * D].T, wk[:, 0:D].T, wk[:, D:2 * D].T, as_np(L0_attn_w_v)], axis=1)
    lambdas = np.stack([as_np(a) for a in (L0_attn_lambda_q1, L0_attn_lambda_k1, L0_attn_lambda_q2, L0_attn_lambda_k2)])
    ins = {"x_in": as_np(L0_attn_x).reshape(T, D), "w_units": w_units, "cols_in": cols,
           "gate_b": as_np(L0_ffn_gate_b)[None, :], "b2_rows": b2_rows, "attn_w": attn_w, "lambdas": lambdas}
    ins = {k: np.ascontiguousarray(a) for k, a in ins.items()}

    nc = bacc.Bacc("TRN2", target_bir_lowering=False, num_devices=1)
    args = [nc.dram_tensor(k, a.shape, mybir.dt.from_np(a.dtype), kind="ExternalInput").ap() for k, a in ins.items()]
    result = nc.dram_tensor("result", (T, D), F32, kind="ExternalOutput").ap()
    macaron(nc, *args, result)
    r = run_bass_kernel_spmd(nc, [ins], core_ids=[0])
    return r.results[0]["result"].reshape(B, T, D)
```

```python
from contextlib import ExitStack

import concourse.bass as bass
from concourse import mybir
from concourse.alu_op_type import AluOpType as ALU

F32 = mybir.dt.float32
F32R = mybir.dt.float32r
ACT = mybir.ActivationFunctionType
AX_X = mybir.AxisListType.X

P = 128


def macaron(nc, x_in, w_units, cols_in, gate_b, b2_rows, attn_w, lambdas, out):
    T, D = x_in.shape
    E = gate_b.shape[1]
    NT = T // P
    BT = 4
    BLK = BT * P
    NB = NT // BT
    NU = w_units.shape[1] // (3 * P)
    NSH = NU - E
    GT_ = 2
    GRP = GT_ * P
    NG = NT // GT_
    CH = BLK
    NCH = T // CH
    HALF = T // 2
    assert D == P and T == NB * BLK and NCH == 4 and NB * 2 == NG
    SCALE = float(D) ** -0.25
    EPS = 1e-5
    LAMBDA_INIT = 0.8
    LAG = 3
    HR = 4
    WR = 3
    WCH = 2
    NWC = NU // WCH
    ONE, LOW = 2 * E, 32
    GR = LOW + E + 1
    BHI, BLO = 2 * E + 1, E + 1

    with ExitStack() as ctx:
        def sb(name, shape, dt=F32):
            return ctx.enter_context(nc.sbuf_tensor(name, shape, dt))

        def sem(name):
            return ctx.enter_context(nc.semaphore(name))

        WORD = 4
        ARENA = (5 * 2 * BT * GRP + (2 * HR + WR + 1) * BLK + 3 * T) * WORD
        ARENA0 = (nc.sbuf_base + 31) // 32 * 32
        sb("arena", [P, ARENA // WORD + 8])

        x = sb("x", [P, NT, D])
        xt_high = [sb(f"xt_high{i}", [P, T], F32R) for i in range(2)]
        xt_low = [sb(f"xt_low{i}", [P, T], F32R) for i in range(2)]
        w_high = sb("w_high", [P, NU, 3, P], F32R)
        w_low = sb("w_low", [P, NU, 3, P], F32R)
        v_high = sb("v_high", [P, NT, D], F32R)
        v_low = sb("v_low", [P, NT, D], F32R)
        gates_t = sb("gates_t", [P, T], F32R)
        gate_rows = sb("gate_rows", [P, (NT - 1) * GR + P])
        pick = sb("pick", [P, E, P], F32R)
        q_high = sb("q_high", [P, 2, 2 * GRP], F32R)
        q_low = sb("q_low", [P, 2, 2 * GRP], F32R)
        a_high = sb("a_high", [P, 2, P], F32R)
        a_low = sb("a_low", [P, 2, P], F32R)
        b2_st = sb("b2_st", [P, P], F32R)
        gw_high = sb("gw_high", [P, E], F32R)
        gw_low = sb("gw_low", [P, E], F32R)
        ident = sb("ident", [P, P])
        cols = sb("cols", [P, 2 * NU + E])
        b1 = lambda u: cols[:, u:u + 1]
        b3 = lambda u: cols[:, NU + u:NU + u + 1]
        gb = sb("gb", [P, E])
        rank = sb("rank", [P, E])
        CONSTS = {"exponent": -0.5, "1/D": 1.0 / D, "EPS": EPS}
        for factor in (1.0, 1.0 - LAMBDA_INIT):
            CONSTS["-0.5", factor] = -0.5 * factor
            CONSTS["1.5", factor] = 1.5 * factor
        consts = sb("consts", [P, len(CONSTS), BT])
        const = {name: consts[:, i, :] for i, name in enumerate(CONSTS)}
        stats = sb("stats", [P, BT, 6])
        mv = sb("mv", [P, BT, 2])
        ve, y0, ya, rstd = (sb(n, [P, BT]) for n in ("ve", "y0", "ya", "rstd"))
        xn = sb("xn", [P, BT, D])
        z, ez, g1, g2 = (sb(n, [P, NT, E]) for n in ("z", "ez", "g1", "g2"))
        g_high = sb("g_high", [P, NT, E], F32R)
        gs = sb("gs", [P, NT])
        lam_s, lam_e = sb("lam_s", [P, 2]), sb("lam_e", [P, 2])
        neg_lam = sb("neg_lam", [P, 1])
        o_s = sb("o_s", [P, GRP])
        o_tok = sb("o_tok", [P, GT_, D])
        ssq, f1, f2, f3, ft = (sb(n, [P, GT_]) for n in ("ssq", "f1", "f2", "f3", "ft"))
        maxes = sb("maxes", [P, NCH])
        neg_m = sb("neg_m", [P, 2, 2])
        sums = sb("sums", [P, 2, 2, NCH])
        total = sb("total", [P, 2])
        r2 = sb("r2", [P, 1])
        r1 = sb("r1", [P, NT])
        neg_c = sb("neg_c", [P, 2])


        def at(name, shape, word, dt=F32):
            size = 1
            for k in shape[1:]:
                size *= k
            assert (word + size) * WORD <= ARENA
            return nc.alloc_sbuf_tensor_at(name, shape, dt, offset=ARENA0 + word * WORD), word + size

        CHUNK = 2 * BT * GRP
        dt_parts, w = at("dt_parts", [P, 7, 2, BT, GRP], 0, F32R)
        assert w == 5 * CHUNK + 2 * HR * BLK
        h_ring, w = at("h_ring", [P, HR, 2, BLK], 5 * CHUNK, F32R)
        gated_ring, w = at("gated_ring", [P, WR, BLK], w)
        out_s, w = at("out_s", [P, BLK], w)
        p_rows, _ = at("p_rows", [P, 3, T], w)
        silu_ring, w = at("silu_ring", [P, 2, BLK], w)
        prod_ring, w = at("prod_ring", [P, 2, BLK], w)
        w_raw, w = at("w_raw", [P, NU, 3, P], 0)
        aw_raw, w = at("aw_raw", [P, 5, P], w)
        aw_high, w = at("aw_high", [P, 5, P], w, F32R)
        aw_low, w = at("aw_low", [P, 5, P], w, F32R)
        b2_raw, w = at("b2_raw", [P, P], w)
        b2_high, w = at("b2_high", [P, P], w, F32R)
        lam_in, w = at("lam_in", [P, 4, D], w)
        lam_prod, w = at("lam_prod", [P, 2, D], w)
        assert w <= 5 * 2 * BT * GRP
        h_high = lambda u: h_ring[:, u % HR, 0, :]
        h_low = lambda u: h_ring[:, u % HR, 1, :]
        silu_s = lambda u: silu_ring[:, u % 2, :]
        prod_s = lambda u: prod_ring[:, u % 2, :]
        gated = lambda u: gated_ring[:, u % WR, :]

        slots = [ctx.enter_context(nc.psum_tensor(f"slot{i}", [P, 2 * BLK], F32)) for i in range(2)]
        bank = {i: ctx.enter_context(nc.psum_tensor(f"bank{i}", [P, BLK], F32)) for i in range(4, 8)}
        single = bank[7]
        ps_h1 = lambda u: slots[0][:, (u % 2) * BLK:(u % 2 + 1) * BLK]
        ps_h3 = lambda u: slots[1][:, (u % 2) * BLK:(u % 2 + 1) * BLK]
        out_bank = lambda b: 4 + b % 2
        gate_bank = lambda ph, b: 5 if (ph, b) == (2, 0) else 7
        FFN_TURN, SIDE_TURN = 6, 5
        dt_bank = lambda c: 4 + 2 * (c % 2)
        score_chunk = lambda c: slots[c // 2][:, (c % 2) * CH:(c % 2 + 1) * CH]
        DVE_TO, POOL_TO = 1, 2
        HALVES = 2 * NT + 1
        TURNED = ("q", "v", "xt", "logits", "o", "gates")

        def diff_done(t, c):
            if c < DVE_TO:
                return dve_diff_ready, t + 1
            steps = POOL_TO - DVE_TO + 1
            return pool_diff_ready, t * steps + min(c, POOL_TO) - DVE_TO + 1

        dt_chunk = lambda g, c: (0, 5, 6, 4)[c] if g % 2 == 0 else c

        x_in_s = [sem(f"x_in{b}") for b in range(NB)]
        w_in_s = [sem(f"w_in{c}") for c in range(NWC)]
        aw_in_s, cols_in_s, gb_in_s, b2_in_s, lam_in_s = (sem(n) for n in ("aw_in", "cols_in", "gb_in", "b2_in", "lam_in_s"))
        out_stored = sem("out_stored")
        pool_const = sem("pool_const")
        w_high_done, w_low_done = sem("w_high_done"), sem("w_low_done")
        gw_high_done, gw_low_done = sem("gw_high_done"), sem("gw_low_done")
        aw_high_done, aw_low_done = sem("aw_high_done"), sem("aw_low_done")
        b2_high_done, b2_low_done = sem("b2_high_done"), sem("b2_low_done")
        turn_full, logits_read = sem("turn_full"), sem("logits_read")
        ve_ready, rstd_ready, xn_ready = sem("ve_ready"), sem("rstd_ready"), sem("xn_ready")
        xt_high_done, xt_low_done = sem("xt_high_done"), sem("xt_low_done")
        z_ready, ez_done, gate_rows_ready, gates_t_done = (sem(n) for n in ("z_ready", "ez_done", "gate_rows_ready", "gates_t_done"))
        h1_full, h3_full, gb_full = sem("h1_full"), sem("h3_full"), sem("gb_full")
        silu_done, prod_done, gated_done = sem("silu_done"), sem("prod_done"), sem("gated_done")
        h_high_done, h_low_done, second_done = sem("h_high_done"), sem("h_low_done"), sem("second_done")
        out_full, out_s_done = sem("out_full"), sem("out_s_done")
        ffn_added, attn_added = sem("ffn_added"), sem("attn_added")
        a_high_done, a_low_done = sem("a_high_done"), sem("a_low_done")
        v_high_done, v_low_done = sem("v_high_done"), sem("v_low_done")
        q_high_done, q_low_done = sem("q_high_done"), sem("q_low_done")
        lam_ready, lam_exp = sem("lam_ready"), sem("lam_exp")
        scores_full, exp_done, neg_m_ready = (sem(n) for n in ("scores_full", "exp_done", "neg_m_ready"))
        neg_c_ready, scaled_done, dve_diff_ready, pool_diff_ready = (sem(n) for n in ("neg_c_ready", "scaled_done", "dve_diff_ready", "pool_diff_ready"))
        dt_high_done, dt_low_done = sem("dt_high_done"), sem("dt_low_done")
        o_full, o_s_done, o_tok_done, ssq_done = (sem(n) for n in ("o_full", "o_s_done", "o_tok_done", "ssq_done"))
        factor_ready = sem("factor_ready")
        dve_chain, pool_chain, gates_t_cleared = sem("dve_chain"), sem("pool_chain"), sem("gates_t_cleared")

        xb = lambda b: x[:, b * BT:(b + 1) * BT, :]
        raw = lambda ap: ap.bitcast(F32)
        use_at = {}

        XT = (0, 1, 0)
        norm_no = lambda ph, b: ph * NB + b
        unit_no = lambda ph, u: (ph // 2) * NB * NU + u
        gated_no = lambda ph, u: (ph // 2) * NB * E + (u // NU) * E + max(u % NU - NSH, 0)
        BATCHES = [(0, 0, BT), (0, BT, BT), (0, 2 * BT, 2 * BT), (2, 0, BT), (2, BT, BT), (2, 2 * BT, 2 * BT)]
        STAGES = 20
        logits_no = lambda ph, b: (ph // 2) * NB + b

        def released(kind, *at):
            if kind == "xt":
                return xt_low_done, norm_no(*at) + 1
            if kind == "logits":
                return logits_read, logits_no(*at) + 1
            if kind == "gates":
                return gates_t_done, (at[0] // 2) * NB + at[1] + 1
            if kind == "out":
                return ffn_added, (at[0] // 2) * NB + at[1] + 1
            if kind == "dt":
                return dt_low_done, NCH * at[0] + at[1] + 1
            done = {"a": a_low_done, "v": v_low_done, "q": q_low_done, "o": o_tok_done}[kind]
            return done, (at[0] if at else 0) + 1

        def turned_behind(t, f):
            d = t - 2 + f
            return d, ((2 * (1 - f), 2 * (1 - f) + 1) if 0 <= d < NT else ())

        FIRST_NORMS = {1: (-1, 1, 3, 5), 2: (2, 4, 6, 8), 3: (5, 7, 9, 13)}
        FIRST_GATES = (1, 11, 21, 23)
        A_STEP = 31
        SPREAD = {0: ((1, 6), (2, 15)), 2: ((4, 1), (5, 16))}

        def attention_side(t, f):
            n = 2 * t + f
            if n == HALVES - 1:
                yield "stages", 4, 0, 2
                yield "exp", 4
            if 1 <= n < NB:
                yield "v", n
            if n % 4 == 0 and n // 4 + 1 < NG:
                yield "q", n // 4 + 1
            for kind, first in (("o", 10), ("add_a", 11), ("add_b", 12)):
                g, r = divmod(n - first, 2 * GT_)
                if r == 0 and 0 <= g < NG:
                    yield kind, g
            for kind, first in (("norm_a", 17), ("norm_b", 19), ("xt", 21), ("logits", 23)):
                b, r = divmod(n - first, 2 * BT)
                if r == 0 and 0 <= b < NB:
                    yield kind, 2, b
            if n == 24:
                yield "stages", 3, 0, 2
                yield "exp", 3
            if n in (25, 27, 29):
                first = 2 + 3 * (n - 25)
                yield "stages", 3, first, first + 6
            if n == 31:
                yield "gates", 2, 0

        def side(ph, s):
            if ph == 0:
                if s == 0:
                    yield "stages", 0, 14, STAGES
                if s in (1, 3, 5):
                    yield "weights", (s + 3) // 2
                if s == 4:
                    yield "lambda_sums",
                if s == 12:
                    yield "attention_weights",
                if s == A_STEP:
                    yield "a",
                for b, steps in FIRST_NORMS.items():
                    if s in steps:
                        yield ("norm_a", "norm_b", "xt", "logits")[steps.index(s)], 0, b
                for k, at in ((1, FIRST_NORMS[1][3]), (2, FIRST_NORMS[3][3])):
                    if s == at:
                        yield "stages", k, 0, 2
                        yield "exp", k
                if s in FIRST_GATES:
                    yield "gates", 0, FIRST_GATES.index(s)
            if ph == 2:
                if HALVES + s < 2 * NT + 16:
                    t, f = divmod(HALVES + s, 2)
                    yield "attention", t, f
                if s == 15:
                    yield "stages", 5, 0, 2
                    yield "exp", 5
                if s in (9, 21, 23):
                    yield "gates", 2, 1 + (9, 21, 23).index(s)
            for b in range(NB):
                first = NU * (b + 1) + LAG
                steps = (first, first + 2, first + 2, first + 4, first + 6)
                if b == NB - 1:
                    steps = (first, first, first + 1, first + 2)
                for kind, at in zip(("out_s", "out", "norm_a", "norm_b", "xt"), steps):
                    if s == at and kind in ("out_s", "out"):
                        yield kind, ph, b
                    elif s == at and ph == 0:
                        yield kind, 1, b
            if ph == 0:
                if s == NB * NU + LAG + 1:
                    yield "q", 0
                if s == NB * NU + LAG + 2:
                    yield "v", 0

        def spread_stages(ph, s, place):
            for k, first in SPREAD[ph]:
                i = 4 * (s - first) + place + 2
                if 2 <= i < STAGES:
                    yield k, i

        FFN_STEPS = {0: NB * NU + LAG + 3, 2: NB * NU + LAG + 1}

        block = ctx.enter_context(nc.Block())

        @block.tensor
        def _(pe):
            last_use = {}

            def bank_free(i):
                if i in last_use:
                    pe.wait_ge(*released(*last_use[i]))

            def use(i, *name):
                bank_free(i)
                use_at[name] = len(use_at), i
                last_use[i] = name
                return bank[i]

            def three(o_ap, stationary, moving, start=True, stop=True):
                (sh, sl), (mh, ml) = stationary, moving
                nc.tensor.matmul(o_ap, sh, mh, start=start, stop=False)
                nc.tensor.matmul(o_ap, sl, mh, start=False, stop=False)
                return nc.tensor.matmul(o_ap, sh, ml, start=False, stop=stop)

            def turn(ps, src, n):
                for j in range(n):
                    last = nc.tensor.transpose(ps[:, j * P:(j + 1) * P], src(j), ident[:])
                last.then_inc(turn_full, 1)

            def wait_xt(ph, b):
                pe.wait_ge(xt_high_done, norm_no(ph, b) + 1)
                pe.wait_ge(xt_low_done, norm_no(ph, b) + 1)

            def xt_parts(ph, a, n):
                return xt_high[XT[ph]][:, a:a + n], xt_low[XT[ph]][:, a:a + n]

            def side_work(i, kind, *at):
                if kind == "xt":
                    ps = use(i, "xt", *at)
                    pe.wait_ge(xn_ready, norm_no(*at) + 1)
                    turn(ps, lambda j: xn[:, j, :], BT)
                if kind == "logits":
                    ph, b = at
                    ps = use(i, "logits", *at)
                    wait_xt(ph, b)
                    for j in range(BT):
                        last = three(ps[:, j * E:(j + 1) * E], xt_parts(ph, (b * BT + j) * P, P), (gw_high[:], gw_low[:]))
                    last.then_inc(turn_full, 1)
                if kind == "gates":
                    ph, b = at
                    ps = use(i, "gates", *at)
                    k = [k for k, (p, t0, n) in enumerate(BATCHES) if p == ph and t0 <= b * BT < t0 + n][0]
                    pe.wait_ge(gate_rows_ready, k + 1)
                    turn(ps, lambda j: gate_rows[:, (b * BT + j) * GR:(b * BT + j) * GR + P], BT)
                if kind == "out":
                    ps = use(i, "out", *at)
                    pe.wait_ge(out_s_done, (at[0] // 2) * NB + at[1] + 1)
                    turn(ps, lambda j: out_s[:, j * P:(j + 1) * P], BT)
                if kind == "a":
                    ps = use(i, "a")
                    pe.wait_ge(aw_low_done, 1)
                    for h in range(2):
                        last = three(ps[:, h * P:(h + 1) * P], (aw_high[:, h, :], aw_low[:, h, :]),
                                     (aw_high[:, 2 + h, :], aw_low[:, 2 + h, :]))
                    last.then_inc(turn_full, 1)
                if kind == "v":
                    b, = at
                    ps = use(i, "v", b)
                    wait_xt(1, b)
                    for j in range(BT):
                        last = three(ps[:, j * P:(j + 1) * P], xt_parts(1, (b * BT + j) * P, P),
                                     (aw_high[:, 4, :], aw_low[:, 4, :]))
                    last.then_inc(turn_full, 1)
                if kind == "q":
                    g, = at
                    ps = use(i, "q", g)
                    wait_xt(1, g // 2)
                    pe.wait_ge(a_low_done, 1)
                    for h in range(2):
                        last = three(ps[:, h * GRP:(h + 1) * GRP], (a_high[:, h, :], a_low[:, h, :]),
                                     xt_parts(1, g * GRP, GRP))
                    last.then_inc(turn_full, 1)
                if kind == "o":
                    g, = at
                    ps = use(i, "o", g)
                    turn(ps, lambda j: o_s[:, j * P:(j + 1) * P], GT_)
                if kind == "attention":
                    attention_half(i, *at)

            def ffn(ph):
                for s in range(FFN_STEPS[ph]):
                    b, e = divmod(s, NU)
                    n = unit_no(ph, s)
                    if s < NB * NU:
                        xt_block = xt_parts(ph, b * BLK, BLK)
                        if ph == 0 and b == 0 and e % WCH == 0:
                            pe.wait_ge(w_low_done, e // WCH + 1)
                        if e == 0:
                            wait_xt(ph, b)
                        if ph == 2 and s < 2:
                            pe.wait_ge(exp_done, NCH * (2 * NT - 1) + s + 1)
                        elif n >= 2:
                            pe.wait_ge(silu_done, n - 1)
                        three(ps_h1(n), (w_high[:, e, 0, :], w_low[:, e, 0, :]), xt_block).then_inc(h1_full, 1)
                        if ph == 2 and s < 2:
                            pe.wait_ge(exp_done, NCH * (2 * NT - 1) + s + 3)
                        elif n >= 2:
                            pe.wait_ge(prod_done, n - 1)
                        three(ps_h3(n), (w_high[:, e, 1, :], w_low[:, e, 1, :]), xt_block).then_inc(h3_full, 1)
                    r = s - LAG
                    if 0 <= r < NB * NU:
                        rb, re = divmod(r, NU)
                        rn = unit_no(ph, r)
                        ps = bank[out_bank(rb)]
                        if re == 0:
                            ob = (ph // 2) * NB + rb
                            if (ph, rb) == (2, 0):
                                bank_free(out_bank(0))
                            elif (ph, rb) == (2, 1):
                                pe.wait_ge(gated_done, gated_no(2, NU))
                            elif ob >= 2:
                                pe.wait_ge(out_s_done, ob - 1)
                        pe.wait_ge(h_high_done, rn + 1)
                        pe.wait_ge(h_low_done, rn + 1)
                        three(ps[:], (w_high[:, re, 2, :], w_low[:, re, 2, :]), (h_high(rn), h_low(rn)),
                              start=(re == 0), stop=False).then_inc(second_done, 1)
                        if re == NU - 1:
                            if (ph, rb) == (0, 0):
                                pe.wait_ge(b2_low_done, 1)
                            nc.tensor.matmul(ps[:], b2_st[:], gates_t[:, rb * BLK:(rb + 1) * BLK],
                                             start=False, stop=True).then_inc(out_full, 1)
                    if s < NB * NU and e >= NSH:
                        g = gated_no(ph, s)
                        i = gate_bank(ph, b)
                        if e == NSH:
                            pe.wait_ge(gates_t_done, (ph // 2) * NB + b + 1)
                            bank_free(i)
                        if (ph, b, e) == (0, 0, NSH):
                            pe.wait_ge(pool_const, 8)
                        if (ph, b, e) == (2, 1, NSH):
                            pe.wait_ge(o_s_done, NG)
                        if g:
                            pe.wait_ge(gated_done, g)
                        nc.tensor.matmul(bank[i][:], pick[:, e - NSH, :], gates_t[:, b * BLK:(b + 1) * BLK],
                                         start=True, stop=True).then_inc(gb_full, 1)
                    for work in side(ph, s):
                        side_work(FFN_TURN, *work)

            def scores(t, h):
                g = (t // GT_) % 2
                a = h * GRP + (t % GT_) * P
                if h == 0 and t % GT_ == 0:
                    pe.wait_ge(q_high_done, t // GT_ + 1)
                    pe.wait_ge(q_low_done, t // GT_ + 1)
                for c in range(NCH):
                    if 2 * t + h >= 1:
                        pe.wait_ge(exp_done, NCH * (2 * t + h - 1) + c + 1)
                    if (t, h, c) == (0, 0, 2):
                        side_work(FFN_TURN, "xt", 1, NB - 1)
                    if (t, h, c) == (0, 0, 3):
                        wait_xt(1, NB - 1)
                    three(score_chunk(c), (q_high[:, g, a:a + P], q_low[:, g, a:a + P]),
                          xt_parts(1, c * CH, CH)).then_inc(scores_full, 1)

            def times_v(g, c):
                if c == 0:
                    if g:
                        pe.wait_ge(o_s_done, g)
                    if g == 0:
                        pe.wait_ge(v_high_done, NB)
                        pe.wait_ge(v_low_done, NB)
                pe.wait_ge(dt_high_done, NCH * (GT_ * g + 1) + c + 1)
                pe.wait_ge(dt_low_done, NCH * (GT_ * g + 1) + c + 1)
                for j in range(BT):
                    k = BT * c + j
                    last = three(single[:, 0:GRP], (v_high[:, k, :], v_low[:, k, :]),
                                 (dt_parts[:, dt_chunk(g, c), 0, j, :], dt_parts[:, dt_chunk(g, c), 1, j, :]),
                                 start=(k == 0), stop=(k == NT - 1))
                if c == NCH - 1:
                    last.then_inc(o_full, 1)

            def attention_half(i, t, f):
                d, chunks = turned_behind(t, f)
                for c in chunks:
                    ps = use(dt_bank(c), "dt", d, c)
                    pe.wait_ge(*diff_done(d, c))
                    turn(ps, lambda j: p_rows[:, d % 2, (BT * c + j) * P:(BT * c + j + 1) * P], BT)
                g, c = divmod(2 * t + f - 6, NCH)
                if 0 <= g < NG:
                    times_v(g, c)
                for work in attention_side(t, f):
                    if work[0] == "o":
                        pe.wait_ge(o_s_done, work[1] + 1)
                    side_work(i, *work)

            pe.wait_ge(pool_const, 2)
            side_work(FFN_TURN, "xt", 0, 0)
            pe.wait_ge(gw_low_done, 1)
            side_work(FFN_TURN, "logits", 0, 0)
            ffn(0)
            for n in range(HALVES):
                t, f = divmod(n, 2)
                if t < NT:
                    scores(t, f)
                attention_half(SIDE_TURN, t, f)
            ffn(2)

        def turned(eng, *name):
            k, i = use_at[name]
            eng.wait_ge(turn_full, k + 1)
            return bank[i]

        @block.scalar
        def _(act):
            def copy(o_ap, i_ap, scale=1.0):
                return nc.scalar.activation(o_ap, i_ap, ACT.Copy, scale=scale)

            def weights(c):
                act.wait_ge(w_in_s[c], 16)
                copy(w_high[:, c * WCH:(c + 1) * WCH, :, :], w_raw[:, c * WCH:(c + 1) * WCH, :, :]).then_inc(w_high_done, 1)

            def side_work(kind, *at):
                if kind == "weights":
                    weights(*at)
                if kind == "attention_weights":
                    act.wait_ge(aw_in_s, 16)
                    copy(aw_high[:], aw_raw[:]).then_inc(aw_high_done, 1)
                if kind == "xt":
                    ph, b = at
                    ps = turned(act, "xt", ph, b)
                    copy(xt_high[XT[ph]][:, b * BLK:(b + 1) * BLK], ps[:]).then_inc(xt_high_done, 1)
                if kind == "exp":
                    k, = at
                    _, t0, n = BATCHES[k]
                    act.wait_ge(z_ready, k + 1)
                    nc.scalar.activation(ez[:, t0:t0 + n, :], z[:, t0:t0 + n, :], ACT.Exp).then_inc(ez_done, 1)
                    if k == 2:
                        act.wait_ge(lam_ready, 1)
                        nc.scalar.activation(lam_e[:], lam_s[:], ACT.Exp).then_inc(lam_exp, 1)
                if kind == "gates":
                    ph, b = at
                    ps = turned(act, "gates", ph, b)
                    if (ph, b) == (0, 0):
                        act.wait_ge(gates_t_cleared, 1)
                    copy(gates_t[0:GR, b * BLK:(b + 1) * BLK], ps[0:GR, :]).then_inc(gates_t_done, 1)
                if kind == "a":
                    ps = turned(act, "a")
                    copy(a_high[:].rearrange("p h c -> p (h c)"), ps[:, 0:2 * P], scale=SCALE).then_inc(a_high_done, 1)
                if kind == "out_s":
                    ph, b = at
                    ob = (ph // 2) * NB + b
                    act.wait_ge(out_full, ob + 1)
                    if ob:
                        act.wait_ge(ffn_added, ob)
                    copy(out_s[:], bank[out_bank(b)][:], scale=0.5).then_inc(out_s_done, 1)
                if kind == "v":
                    b, = at
                    ps = turned(act, "v", b)
                    copy(v_high[:, b * BT:(b + 1) * BT, :], ps[:].rearrange("p (t d) -> p t d", t=BT)).then_inc(v_high_done, 1)
                if kind == "q":
                    g, = at
                    ps = turned(act, "q", g)
                    copy(q_high[:, g % 2, :], ps[:]).then_inc(q_high_done, 1)
                if kind == "o":
                    g, = at
                    ps = turned(act, "o", g)
                    if g:
                        act.wait_ge(attn_added, g)
                    copy(o_tok[:].rearrange("p t d -> p (t d)"), ps[:, 0:GRP]).then_inc(o_tok_done, 1)
                    act.wait_ge(o_tok_done, g + 1)
                    for j in range(GT_):
                        if j:
                            act.wait_ge(ssq_done, GT_ * g + j)
                        nc.scalar.activation(o_s[:, 0:D], o_tok[:, j, :], ACT.Square,
                                             accum_out=ssq[:, j:j + 1]).then_inc(ssq_done, 1)
                if kind == "attention":
                    attention_half(*at)

            def ffn(ph):
                for s in range(FFN_STEPS[ph]):
                    n = unit_no(ph, s)
                    if s < NB * NU:
                        act.wait_ge(h1_full, n + 1)
                        if n >= 2:
                            act.wait_ge(prod_done, n - 1)
                        if (ph, s) == (2, 0):
                            act.wait_ge(turn_full, use_at["dt", NT - 2, 1][0] + 1)
                        nc.scalar.activation(silu_s(n), ps_h1(n), ACT.Silu, bias=b1(s % NU)).then_inc(silu_done, 1)
                    r = s - 1
                    if 0 <= r < NB * NU:
                        rn = unit_no(ph, r)
                        if r % NU < NSH:
                            act.wait_ge(prod_done, rn + 1)
                        else:
                            act.wait_ge(gated_done, gated_no(ph, r) + 1)
                        if rn >= HR:
                            act.wait_ge(second_done, rn - HR + 1)
                        copy(h_high(rn), gated(rn)).then_inc(h_high_done, 1)
                    for work in side(ph, s):
                        side_work(*work)

            def dt_copy(t, c):
                ps = turned(act, "dt", t, c)
                q = slice((t % GT_) * P, (t % GT_ + 1) * P)
                copy(dt_parts[:, dt_chunk(t // GT_, c), 0, :, q], ps[:].rearrange("p (k q) -> p k q", k=BT)).then_inc(dt_high_done, 1)

            def exp(t, h, c):
                if t >= NT:
                    return
                if c == 0:
                    act.wait_ge(neg_m_ready, 2 * t + h + 1)
                if h == 0 and t >= 2:
                    act.wait_ge(turn_full, use_at["dt", t - 2, c][0] + 1)
                if h == 1 and t >= 1:
                    act.wait_ge(*diff_done(t - 1, c))
                keys = slice(c * CH, (c + 1) * CH)
                nc.scalar.activation(p_rows[:, 2 if h else t % 2, keys], score_chunk(c),
                                     ACT.Exp, bias=neg_m[:, t % 2, h:h + 1],
                                     accum_out=sums[:, t % 2, h, c:c + 1]).then_inc(exp_done, 1)

            def attention_half(t, f):
                if f == 0 and 1 <= t <= NT:
                    keys = slice(POOL_TO * CH, T)
                    act.wait_ge(neg_c_ready, t)
                    act.wait_ge(exp_done, NCH * 2 * t)
                    copy(p_rows[:, 2, keys], p_rows[:, 2, keys],
                         scale=neg_c[:, (t - 1) % 2:(t - 1) % 2 + 1]).then_inc(scaled_done, 1)
                d, chunks = turned_behind(t, f)
                for c in chunks:
                    dt_copy(d, c)
                for c in range(NCH):
                    exp(t, f, c)
                g, c = divmod(2 * t + f - 6, NCH)
                if 0 <= g < NG and c == NCH - 1:
                    act.wait_ge(o_full, g + 1)
                    if g:
                        act.wait_ge(ssq_done, GT_ * g)
                    copy(o_s[:], single[:, 0:GRP]).then_inc(o_s_done, 1)
                for work in attention_side(t, f):
                    side_work(*work)

            act.wait_ge(cols_in_s, 16)
            copy(gw_high[:], cols[:, 2 * NU:2 * NU + E]).then_inc(gw_high_done, 1)
            weights(0)
            weights(1)
            act.wait_ge(b2_in_s, 32)
            act.wait_ge(pool_const, 5)
            copy(b2_st[0:BHI, :], b2_raw[0:BHI, :]).then_inc(b2_high_done, 1)
            copy(b2_high[LOW:LOW + BLO, :], b2_raw[LOW:LOW + BLO, :]).then_inc(b2_high_done, 1)
            side_work("xt", 0, 0)
            side_work("exp", 0)
            ffn(0)
            side_work("xt", 1, NB - 1)
            for n in range(HALVES):
                attention_half(*divmod(n, 2))
            ffn(2)

        @block.gpsimd
        def _(pool):
            nc.gpsimd.memset(ident[:], 0.0).then_inc(pool_const, 1)
            pool.wait_ge(pool_const, 1)
            nc.gpsimd.affine_select(out=ident[:], in_=ident[:], compare_op=ALU.not_equal, fill=1.0, base=0,
                                    pattern=[[-1, P]], channel_multiplier=1).then_inc(pool_const, 1)
            for name in CONSTS:
                last = nc.gpsimd.memset(const[name], CONSTS[name])
            last.then_inc(pool_const, 1)
            count = [0]

            def then(ins):
                count[0] += 1
                ins.then_inc(pool_chain, 1)
                pool.wait_ge(pool_chain, count[0])

            def minus_half(v, y, t, factor, o_ap):
                n = v.shape[1]
                mul = lambda a, b, c: nc.gpsimd.tensor_tensor(a, b, c, ALU.mult)
                then(nc.gpsimd.tensor_tensor(y, v, const["exponent"][:, 0:n], ALU.pow))
                then(mul(t, y, y))
                then(mul(t, t, v))
                then(mul(t, t, const["-0.5", factor][:, 0:n]))
                then(nc.gpsimd.tensor_tensor(t, t, const["1.5", factor][:, 0:n], ALU.add))
                return mul(o_ap, y, t)

            def low(dst, src, high):
                return nc.gpsimd.tensor_tensor(dst, src, raw(high), ALU.subtract)

            def weights(c):
                pool.wait_ge(w_high_done, c + 1)
                u = slice(c * WCH, (c + 1) * WCH)
                low(w_low[:, u, :, :], w_raw[:, u, :, :], w_high[:, u, :, :]).then_inc(w_low_done, 1)

            def side_work(kind, *at):
                if kind == "norm_a":
                    k = norm_no(*at)
                    pool.wait_ge(ve_ready, k + 1)
                    if k:
                        pool.wait_ge(xn_ready, k)
                    minus_half(ve[:], y0[:], ya[:], 1.0, rstd[:]).then_inc(rstd_ready, 1)
                if kind == "add_a":
                    g, = at
                    r = r1[:, g * GT_:(g + 1) * GT_]
                    pool.wait_ge(ssq_done, GT_ * (g + 1))
                    pool.wait_ge(neg_c_ready, GT_ * (g + 1))
                    if g:
                        pool.wait_ge(attn_added, g)
                    then(nc.gpsimd.tensor_tensor(f1[:], r, r, ALU.mult))
                    then(nc.gpsimd.tensor_tensor(f1[:], f1[:], ssq[:], ALU.mult))
                    then(nc.gpsimd.tensor_tensor(f1[:], f1[:], const["1/D"][:, 0:GT_], ALU.mult))
                    then(nc.gpsimd.tensor_tensor(f1[:], f1[:], const["EPS"][:, 0:GT_], ALU.add))
                    then(minus_half(f1[:], f2[:], ft[:], 1.0 - LAMBDA_INIT, f3[:]))
                    nc.gpsimd.tensor_tensor(f3[:], f3[:], r, ALU.mult).then_inc(factor_ready, 1)
                if kind == "weights":
                    weights(*at)
                if kind == "attention_weights":
                    pool.wait_ge(aw_high_done, 1)
                    low(aw_low[:], aw_raw[:], aw_high[:]).then_inc(aw_low_done, 1)
                if kind == "attention":
                    attention_half(*at)

            def attention_half(t, f):
                if f == 0 and 1 <= t <= NT:
                    i = (t - 1) % 2
                    pool.wait_ge(neg_c_ready, t)
                    for c in range(DVE_TO, POOL_TO):
                        keys = slice(c * CH, (c + 1) * CH)
                        then(nc.gpsimd.tensor_tensor(p_rows[:, 2, keys], p_rows[:, 2, keys],
                                                     neg_c[:, i:i + 1].to_broadcast([P, CH]), ALU.mult))
                        nc.gpsimd.tensor_tensor(p_rows[:, i, keys], p_rows[:, i, keys], p_rows[:, 2, keys],
                                                ALU.add).then_inc(pool_diff_ready, 1)
                    pool.wait_ge(scaled_done, t)
                    keys = slice(POOL_TO * CH, T)
                    nc.gpsimd.tensor_tensor(p_rows[:, i, keys], p_rows[:, i, keys], p_rows[:, 2, keys],
                                            ALU.add).then_inc(pool_diff_ready, 1)
                for work in attention_side(t, f):
                    side_work(*work)

            def ffn(ph):
                for s in range(FFN_STEPS[ph]):
                    r = s - 1
                    if 0 <= r < NB * NU:
                        rn = unit_no(ph, r)
                        pool.wait_ge(h_high_done, rn + 1)
                        low(h_low(rn), gated(rn), h_high(rn)).then_inc(h_low_done, 1)
                    for work in side(ph, s):
                        side_work(*work)

            nc.gpsimd.memset(gate_rows[:], 1.0).then_inc(pool_const, 1)
            nc.gpsimd.memset(raw(b2_st[:]), 0.0).then_inc(pool_const, 1)
            nc.gpsimd.memset(raw(pick[:]), 0.0).then_inc(pool_const, 1)
            pool.wait_ge(pool_const, 3)
            side_work("norm_a", 0, 0)
            pool.wait_ge(gw_high_done, 1)
            low(gw_low[:], cols[:, 2 * NU:2 * NU + E], gw_high[:]).then_inc(gw_low_done, 1)
            weights(0)
            for i, first in enumerate((0, E)):
                pool.wait_ge(pool_const, 6 + i)
                nc.gpsimd.affine_select(out=pick[:], in_=raw(pick[:]), compare_op=ALU.not_equal, fill=1.0, base=-first,
                                        pattern=[[-1, E], [0, P]], channel_multiplier=1).then_inc(pool_const, 1)
            side_work("norm_a", 0, 1)
            weights(1)
            ffn(0)
            for n in range(HALVES):
                attention_half(*divmod(n, 2))
            ffn(2)

        @block.vector
        def _(dve):
            count = [0]
            last_of = {}

            def did(chain, ins):
                count[0] += 1
                ins.then_inc(dve_chain, 1)
                last_of[chain] = count[0]

            def after(chain):
                dve.wait_ge(dve_chain, last_of[chain])

            def low(dst, src, high):
                return nc.vector.tensor_tensor(dst, src, raw(high), ALU.subtract)

            def best(part, src, top, marks, sel):
                n = src.shape[1]
                over = top.unsqueeze(2).to_broadcast([P, n, E])
                ranks = rank[:].unsqueeze(1).to_broadcast([P, n, E])
                if part == 0:
                    return nc.vector.tensor_reduce(top, src, AX_X, ALU.max)
                if part == 1:
                    return nc.vector.tensor_tensor(marks, src, over, ALU.is_equal)
                if part == 2:
                    return nc.vector.tensor_tensor(marks, marks, ranks, ALU.mult)
                if part == 3:
                    return nc.vector.tensor_reduce(top, marks, AX_X, ALU.max)
                return nc.vector.tensor_tensor(sel, marks, over, ALU.is_equal)

            def gate_stage(k, i):
                ph, t0, n = BATCHES[k]
                a, b, z_, ez_, hi = (m[:, t0:t0 + n, :] for m in (g1, g2, z, ez, g_high))
                top = gs[:, t0:t0 + n]
                over = top.unsqueeze(2).to_broadcast([P, n, E])
                if i == 0:
                    dve.wait_ge(logits_read, logits_no(ph, (t0 + n) // BT - 1) + 1)
                    did("gate", nc.vector.tensor_reduce(top, a, AX_X, ALU.max))
                    return
                after("gate")
                if i == 1:
                    nc.vector.tensor_tensor(z_, a, over, ALU.subtract).then_inc(z_ready, 1)
                    return
                if i == 2:
                    dve.wait_ge(z_ready, k + 1)
                    dve.wait_ge(ez_done, k + 1)
                    did("gate", nc.vector.tensor_reduce(top, ez_, AX_X, ALU.add))
                if i == 3:
                    did("gate", nc.vector.reciprocal(top, top))
                if i == 4:
                    did("gate", nc.vector.tensor_tensor(a, ez_, over, ALU.mult))
                if 5 <= i < 10:
                    did("gate", best(i - 5, a, top, b, b))
                if i == 10:
                    did("gate", nc.vector.scalar_tensor_tensor(ez_, b, -2.0, a, ALU.mult, ALU.add))
                if 11 <= i < 16:
                    did("gate", best(i - 11, ez_, top, z_, z_))
                if i == 16:
                    did("gate", nc.vector.tensor_tensor(b, b, z_, ALU.add))
                if i == 17:
                    did("gate", nc.vector.tensor_tensor(a, a, b, ALU.mult))
                if i == 18:
                    did("gate", nc.vector.tensor_copy(hi, a))
                if i == 19:
                    rows = gate_rows[:, t0 * GR:(t0 + n) * GR].rearrange("p (t r) -> p t r", r=GR)
                    nc.vector.tensor_copy(rows[:, :, 0:E], raw(hi))
                    nc.vector.tensor_copy(rows[:, :, LOW:LOW + E], raw(hi))
                    nc.vector.tensor_tensor(rows[:, :, E:2 * E], a, raw(hi), ALU.subtract).then_inc(gate_rows_ready, 1)

            def side_work(kind, *at):
                if kind == "norm_a":
                    ph, b = at
                    if ph == 0:
                        dve.wait_ge(x_in_s[b], 16)
                    if ph == 1:
                        dve.wait_ge(ffn_added, b + 1)
                    if ph == 2:
                        dve.wait_ge(attn_added, 2 * (b + 1))
                    for j in range(BT):
                        last = nc.vector.bn_stats(stats[:, j, :], x[:, b * BT + j, :])
                    did("norm", last)
                    after("norm")
                    for j in range(BT):
                        last = nc.vector.bn_aggr(mv[:, j, :], stats[:, j, :])
                    did("norm", last)
                    after("norm")
                    nc.vector.tensor_scalar(ve[:], mv[:, :, 1], EPS, None, ALU.add).then_inc(ve_ready, 1)
                if kind == "norm_b":
                    ph, b = at
                    k = norm_no(ph, b)
                    dve.wait_ge(rstd_ready, k + 1)
                    if k:
                        dve.wait_ge(xt_high_done, k)
                    for j in range(BT):
                        last = nc.vector.tensor_scalar(xn[:, j, :], x[:, b * BT + j, :], mv[:, j, 0:1], rstd[:, j:j + 1],
                                                       ALU.subtract, ALU.mult)
                    last.then_inc(xn_ready, 1)
                if kind == "xt":
                    ph, b = at
                    tok = slice(b * BLK, (b + 1) * BLK)
                    ps = turned(dve, "xt", ph, b)
                    dve.wait_ge(xt_high_done, norm_no(ph, b) + 1)
                    low(xt_low[XT[ph]][:, tok], ps[:], xt_high[XT[ph]][:, tok]).then_inc(xt_low_done, 1)
                if kind == "logits":
                    ph, b = at
                    ps = turned(dve, "logits", ph, b)
                    if (ph, b) == (0, 0):
                        dve.wait_ge(gb_in_s, 16)
                    nc.vector.tensor_tensor(g1[:, b * BT:(b + 1) * BT, :], ps[:, 0:BT * E].rearrange("p (t e) -> p t e", e=E),
                                            gb[:].unsqueeze(1).to_broadcast([P, BT, E]), ALU.add).then_inc(logits_read, 1)
                if kind == "stages":
                    k, lo, hi = at
                    if (k, lo) == (0, 2):
                        dve.wait_ge(pool_const, 4)
                    for i in range(lo, hi):
                        gate_stage(k, i)
                if kind == "lambda_sums":
                    dve.wait_ge(lam_in_s, 16)
                    did("lambda", nc.vector.tensor_tensor(lam_prod[:], lam_in[:, 0:4:2, :], lam_in[:, 1:4:2, :], ALU.mult))
                    after("lambda")
                    nc.vector.tensor_reduce(lam_s[:], lam_prod[:], AX_X, ALU.add).then_inc(lam_ready, 1)
                if kind == "a":
                    dve.wait_ge(lam_exp, 1)
                    did("lambda", nc.vector.tensor_tensor(neg_lam[:], lam_e[:, 1:2], lam_e[:, 0:1], ALU.subtract))
                    after("lambda")
                    did("lambda", nc.vector.tensor_scalar(neg_lam[:], neg_lam[:], -LAMBDA_INIT, None, ALU.add))
                    ps = turned(dve, "a")
                    dve.wait_ge(a_high_done, 1)
                    nc.vector.scalar_tensor_tensor(a_low[:].rearrange("p h c -> p (h c)"), ps[:, 0:2 * P], SCALE,
                                                   raw(a_high[:].rearrange("p h c -> p (h c)")),
                                                   ALU.mult, ALU.subtract).then_inc(a_low_done, 1)
                if kind == "out":
                    ph, b = at
                    ps = turned(dve, "out", ph, b)
                    flat = xb(b).rearrange("p t d -> p (t d)")
                    nc.vector.tensor_tensor(flat, ps[:], flat, ALU.add).then_inc(ffn_added, 1)
                if kind == "v":
                    b, = at
                    ps = turned(dve, "v", b)
                    dve.wait_ge(v_high_done, b + 1)
                    low(v_low[:, b * BT:(b + 1) * BT, :], ps[:].rearrange("p (t d) -> p t d", t=BT),
                        v_high[:, b * BT:(b + 1) * BT, :]).then_inc(v_low_done, 1)
                if kind == "q":
                    g, = at
                    ps = turned(dve, "q", g)
                    dve.wait_ge(q_high_done, g + 1)
                    low(q_low[:, g % 2, :], ps[:], q_high[:, g % 2, :]).then_inc(q_low_done, 1)
                if kind == "add_b":
                    g, = at
                    dve.wait_ge(factor_ready, g + 1)
                    dve.wait_ge(o_tok_done, g + 1)
                    for j in range(GT_):
                        xj = x[:, g * GT_ + j, :]
                        last = nc.vector.scalar_tensor_tensor(xj, o_tok[:, j, :], f3[:, j:j + 1], xj, ALU.mult, ALU.add)
                    last.then_inc(attn_added, 1)
                if kind == "attention":
                    attention_half(*at)

            def gate_stages(ph, s, place):
                for k, i in spread_stages(ph, s, place):
                    gate_stage(k, i)

            def ffn(ph):
                for s in range(FFN_STEPS[ph]):
                    n = unit_no(ph, s)
                    if s < NB * NU:
                        b, e = divmod(s, NU)
                        g = gated_no(ph, s)
                        gate_stages(ph, s, 0)
                        dve.wait_ge(h3_full, n + 1)
                        dve.wait_ge(silu_done, n + 1)
                        if e < NSH and n >= WR:
                            dve.wait_ge(h_low_done, n - WR + 1)
                        nc.vector.scalar_tensor_tensor(gated(n) if e < NSH else prod_s(n), ps_h3(n), b3(e), silu_s(n),
                                                       ALU.add, ALU.mult).then_inc(prod_done, 1)
                        gate_stages(ph, s, 1)
                        if e >= NSH:
                            dve.wait_ge(prod_done, n + 1)
                            dve.wait_ge(gb_full, g + 1)
                            if n >= WR:
                                dve.wait_ge(h_low_done, n - WR + 1)
                            nc.vector.tensor_tensor(gated(n), bank[gate_bank(ph, b)][:], prod_s(n), ALU.mult).then_inc(gated_done, 1)
                        gate_stages(ph, s, 2)
                    for work in side(ph, s):
                        side_work(*work)
                    gate_stages(ph, s, 3)

            def dt_low_part(t, c):
                q = slice((t % GT_) * P, (t % GT_ + 1) * P)
                k = dt_chunk(t // GT_, c)
                ps = turned(dve, "dt", t, c)
                dve.wait_ge(dt_high_done, NCH * t + c + 1)
                low(dt_parts[:, k, 1, :, q], ps[:].rearrange("p (k q) -> p k q", k=BT),
                    dt_parts[:, k, 0, :, q]).then_inc(dt_low_done, 1)

            def chunk_max(t, h, c):
                if c == 0 and 2 * t + h:
                    dve.wait_ge(neg_m_ready, 2 * t + h)
                dve.wait_ge(scores_full, NCH * (2 * t + h) + c + 1)
                did("max", nc.vector.tensor_reduce(maxes[:, c:c + 1], score_chunk(c), AX_X, ALU.max))

            def row_max(t, h):
                after("max")
                nc.vector.tensor_reduce(neg_m[:, t % 2, h:h + 1], maxes[:], AX_X, ALU.max, negate=True).then_inc(neg_m_ready, 1)

            def ratio(t):
                i = t % 2
                dve.wait_ge(exp_done, NCH * 2 * (t + 1))
                did("combine", nc.vector.tensor_reduce(total[:], sums[:, i, :, :], AX_X, ALU.add))
                after("combine")
                did("combine", nc.vector.reciprocal(r2[:], total[:, 1:2]))
                nc.vector.reciprocal(r1[:, t:t + 1], total[:, 0:1])
                if t == 0:
                    after("lambda")
                after("combine")
                nc.vector.tensor_scalar(neg_c[:, i:i + 1], total[:, 0:1], r2[:], neg_lam[:], ALU.mult, ALU.mult).then_inc(neg_c_ready, 1)

            def combine(t):
                dve.wait_ge(neg_c_ready, t + 1)
                nc.vector.scalar_tensor_tensor(p_rows[:, t % 2, 0:DVE_TO * CH], p_rows[:, 2, 0:DVE_TO * CH], neg_c[:, t % 2:t % 2 + 1],
                                               p_rows[:, t % 2, 0:DVE_TO * CH], ALU.mult, ALU.add).then_inc(dve_diff_ready, 1)

            def attention_half(t, f):
                new = f == 0 and 1 <= t <= NT
                if t < NT:
                    chunk_max(t, f, 0)
                if new:
                    ratio(t - 1)
                if t < NT:
                    chunk_max(t, f, 1)
                    chunk_max(t, f, 2)
                    if (t, f) != (0, 0):
                        turned_side(*divmod(2 * t + f - 1, 2))
                    chunk_max(t, f, 3)
                    row_max(t, f)
                if new:
                    combine(t - 1)
                d, chunks = turned_behind(t, f)
                for c in chunks:
                    dt_low_part(d, c)
                for work in attention_side(t, f):
                    if work[0] not in TURNED:
                        side_work(*work)
                if t >= NT or (t, f) == (NT - 1, 1):
                    turned_side(t, f)

            def turned_side(t, f):
                for work in attention_side(t, f):
                    if work[0] in TURNED:
                        side_work(*work)

            for e in range(E):
                last = nc.vector.memset(rank[:, e:e + 1], float(E - e))
            did("gate", last)
            nc.vector.memset(raw(gates_t[:]), 0.0).then_inc(gates_t_cleared, 1)
            side_work("norm_a", 0, 0)
            side_work("norm_b", 0, 0)
            side_work("norm_a", 0, 1)
            side_work("xt", 0, 0)
            dve.wait_ge(b2_high_done, 2)
            low(b2_st[LOW:LOW + BLO, :], b2_raw[LOW:LOW + BLO, :], b2_high[LOW:LOW + BLO, :]).then_inc(b2_low_done, 1)
            side_work("logits", 0, 0)
            side_work("stages", 0, 0, 14)
            ffn(0)
            side_work("xt", 1, NB - 1)
            for n in range(HALVES):
                attention_half(*divmod(n, 2))
            ffn(2)

        @block.sync
        def _(sp):
            x_rows = x_in.rearrange("(t p) d -> p t d", p=P)
            out_rows = out.rearrange("(t p) d -> p t d", p=P)
            w_rows = w_units.rearrange("p (u k c) -> p u k c", k=3, c=P)
            load_x = lambda b: sp.dma_start(xb(b), x_rows[:, b * BT:(b + 1) * BT, :]).then_inc(x_in_s[b], 16)

            def load_weights(c):
                sp.dma_start(w_raw[:, c * WCH:(c + 1) * WCH, :, :], w_rows[:, c * WCH:(c + 1) * WCH, :, :]).then_inc(w_in_s[c], 16)

            load_x(0)
            sp.dma_start(cols[:], cols_in).then_inc(cols_in_s, 16)
            load_weights(0)
            load_x(1)
            sp.dma_start(gb[:], gate_b[0, :].partition_broadcast(P)).then_inc(gb_in_s, 16)
            load_weights(1)
            sp.dma_start(b2_raw[0:BHI, :], b2_rows[0:BHI, :]).then_inc(b2_in_s, 16)
            sp.dma_start(b2_raw[LOW:LOW + BLO, :], b2_rows[BHI:BHI + BLO, :]).then_inc(b2_in_s, 16)
            for b in range(2, NB):
                load_x(b)
            for c in range(2, NWC):
                load_weights(c)
            sp.dma_start(lam_in[:], lambdas.partition_broadcast(P)).then_inc(lam_in_s, 16)
            sp.dma_start(aw_raw[:], attn_w.rearrange("p (k c) -> p k c", c=P)).then_inc(aw_in_s, 16)
            for b in range(NB):
                sp.wait_ge(ffn_added, NB + b + 1)
                sp.dma_start(out_rows[:, b * BT:(b + 1) * BT, :], xb(b)).then_inc(out_stored, 16)
            sp.wait_ge(out_stored, 16 * NB)


def kernel(L0_attn_x, L0_attn_w_q12, L0_attn_w_k12, L0_attn_w_v, L0_attn_lambda_q1, L0_attn_lambda_k1,
           L0_attn_lambda_q2, L0_attn_lambda_k2, L0_ffn_gate_w, L0_ffn_gate_b, L0_ffn_w1, L0_ffn_b1, L0_ffn_w3,
           L0_ffn_b3, L0_ffn_w2, L0_ffn_b2, L0_ffn_ws1, L0_ffn_bs1, L0_ffn_ws3, L0_ffn_bs3, L0_ffn_ws2, L0_ffn_bs2):
    import numpy as np
    import concourse.bacc as bacc
    from concourse.bass_utils import run_bass_kernel_spmd

    B, T, D = L0_attn_x.shape
    S = L0_ffn_ws1.shape[0] // P
    as_np = lambda a: np.asarray(a)
    first = np.concatenate([as_np(L0_ffn_ws1).reshape(S, P, D), as_np(L0_ffn_w1)]).transpose(2, 0, 1)
    third = np.concatenate([as_np(L0_ffn_ws3).reshape(S, P, D), as_np(L0_ffn_w3)]).transpose(2, 0, 1)
    second = np.concatenate([as_np(L0_ffn_ws2).reshape(D, S, P).transpose(1, 0, 2), as_np(L0_ffn_w2)]).transpose(2, 0, 1)
    w_units = np.stack([first, third, second], axis=2).reshape(P, -1)
    b1 = np.concatenate([as_np(L0_ffn_bs1).reshape(S, P), as_np(L0_ffn_b1)]).T
    b3 = np.concatenate([as_np(L0_ffn_bs3).reshape(S, P), as_np(L0_ffn_b3)]).T
    cols = np.concatenate([b1, b3, as_np(L0_ffn_gate_w).T], axis=1)
    b2, bs2 = as_np(L0_ffn_b2), as_np(L0_ffn_bs2)[None, :]
    b2_rows = np.concatenate([b2, b2, bs2, b2, bs2])
    wq, wk = as_np(L0_attn_w_q12), as_np(L0_attn_w_k12)
    attn_w = np.concatenate([wq[:, 0:D].T, wq[:, D:2 * D].T, wk[:, 0:D].T, wk[:, D:2 * D].T, as_np(L0_attn_w_v)], axis=1)
    lambdas = np.stack([as_np(a) for a in (L0_attn_lambda_q1, L0_attn_lambda_k1, L0_attn_lambda_q2, L0_attn_lambda_k2)])
    ins = {"x_in": as_np(L0_attn_x).reshape(T, D), "w_units": w_units, "cols_in": cols,
           "gate_b": as_np(L0_ffn_gate_b)[None, :], "b2_rows": b2_rows, "attn_w": attn_w, "lambdas": lambdas}
    ins = {k: np.ascontiguousarray(a) for k, a in ins.items()}

    nc = bacc.Bacc("TRN2", target_bir_lowering=False, num_devices=1)
    args = [nc.dram_tensor(k, a.shape, mybir.dt.from_np(a.dtype), kind="ExternalInput").ap() for k, a in ins.items()]
    result = nc.dram_tensor("result", (T, D), F32, kind="ExternalOutput").ap()
    macaron(nc, *args, result)
    r = run_bass_kernel_spmd(nc, [ins], core_ids=[0])
    return r.results[0]["result"].reshape(B, T, D)
```
